# Optimizing a Trainium2 kernel written in Bass

```python
import numpy as np
import jax
import jax.numpy as jnp

def _softmax(x, axis=-1):
    return jax.nn.softmax(x, axis=axis)

def _gelu(x):
    return jax.nn.gelu(x, approximate=True)

def _silu(x):
    return jax.nn.silu(x)

def _sigmoid(x):
    return jax.nn.sigmoid(x)

def _layernorm(x, axis=-1, eps=1e-05):
    m = jnp.mean(x, axis=axis, keepdims=True)
    v = jnp.var(x, axis=axis, keepdims=True)
    return (x - m) / jnp.sqrt(v + eps)

def _scatter_add(tgt, idx, src, axis=0):
    return tgt.at[idx].add(src)

def _segment_sum(src, seg, n):
    return jax.ops.segment_sum(src, seg, n)
kernel_name = 'mk_prb_d1_jaxref_r8_8197c9'

def setup_inputs(seed: int=0):
    np.random.seed(seed)
    _w = jnp.asarray

    def _L0_attn_setup():
        import jax, jax.numpy as jnp
        import numpy as np
        D_MODEL = 256
        H = 16
        D_K = D_MODEL // H
        key = jax.random.key(seed)
        ks = jax.random.split(key, 9)
        b, n, d = (2, 256, D_MODEL)
        s = 1.0 / np.sqrt(d)
        return {'x': jax.random.normal(ks[0], (b, n, d), jnp.float32), 'Wq': jax.random.normal(ks[1], (d, d), jnp.float32) * s, 'bq': jax.random.normal(ks[2], (d,), jnp.float32) * 0.01, 'Wk': jax.random.normal(ks[3], (d, d), jnp.float32) * s, 'bk': jax.random.normal(ks[4], (d,), jnp.float32) * 0.01, 'Wv': jax.random.normal(ks[5], (d, d), jnp.float32) * s, 'bv': jax.random.normal(ks[6], (d,), jnp.float32) * 0.01, 'Wo': jax.random.normal(ks[7], (d, d), jnp.float32) * s, 'bo': jax.random.normal(ks[8], (d,), jnp.float32) * 0.01}
    _L0_attn_in = _L0_attn_setup()

    def _L0_ffn_setup():
        import jax, jax.numpy as jnp
        import numpy as np
        H = 256
        E = 16
        K = 4
        I = 176
        IS = 176 * 2
        B, S = (1, 128)
        key = jax.random.key(seed)
        ks = jax.random.split(key, 9)
        scale = 0.02
        return {'hidden_states': jax.random.normal(ks[0], (B, S, H), dtype=jnp.float32), 'gate_w': jax.random.normal(ks[1], (E, H), dtype=jnp.float32) * scale, 'w_gate': jax.random.normal(ks[2], (E, H, I), dtype=jnp.float32) * scale, 'w_up': jax.random.normal(ks[3], (E, H, I), dtype=jnp.float32) * scale, 'w_down': jax.random.normal(ks[4], (E, I, H), dtype=jnp.float32) * scale, 'sw_gate': jax.random.normal(ks[5], (H, IS), dtype=jnp.float32) * scale, 'sw_up': jax.random.normal(ks[6], (H, IS), dtype=jnp.float32) * scale, 'sw_down': jax.random.normal(ks[7], (IS, H), dtype=jnp.float32) * scale}
    _L0_ffn_in = _L0_ffn_setup()
    _d = {'L0_attn_x': _L0_attn_in['x'], 'L0_attn_Wq': _L0_attn_in['Wq'], 'L0_attn_bq': _L0_attn_in['bq'], 'L0_attn_Wk': _L0_attn_in['Wk'], 'L0_attn_bk': _L0_attn_in['bk'], 'L0_attn_Wv': _L0_attn_in['Wv'], 'L0_attn_bv': _L0_attn_in['bv'], 'L0_attn_Wo': _L0_attn_in['Wo'], 'L0_attn_bo': _L0_attn_in['bo'], 'L0_ffn_gate_w': _L0_ffn_in['gate_w'], 'L0_ffn_w_gate': _L0_ffn_in['w_gate'], 'L0_ffn_w_up': _L0_ffn_in['w_up'], 'L0_ffn_w_down': _L0_ffn_in['w_down'], 'L0_ffn_sw_gate': _L0_ffn_in['sw_gate'], 'L0_ffn_sw_up': _L0_ffn_in['sw_up'], 'L0_ffn_sw_down': _L0_ffn_in['sw_down']}
    _x0 = _d['L0_attn_x']
    _d['L0_attn_x'] = jax.random.normal(jax.random.fold_in(jax.random.key(seed), 1), (4, 1024, 256), dtype=_x0.dtype)
    del _x0
    return _d

def reference(L0_attn_x, L0_attn_Wq, L0_attn_bq, L0_attn_Wk, L0_attn_bk, L0_attn_Wv, L0_attn_bv, L0_attn_Wo, L0_attn_bo, L0_ffn_gate_w, L0_ffn_w_gate, L0_ffn_w_up, L0_ffn_w_down, L0_ffn_sw_gate, L0_ffn_sw_up, L0_ffn_sw_down):

    def _L0_attn_ref(x, Wq, bq, Wk, bk, Wv, bv, Wo, bo):
        import jax, jax.numpy as jnp
        import numpy as np
        D_MODEL = 256
        H = 16
        D_K = D_MODEL // H
        b, n, d = x.shape
        h, dk = (H, D_K)

        def split_heads(t):
            return t.reshape(b, n, h, dk).transpose(0, 2, 1, 3)
        q = split_heads(x @ Wq + bq)
        k = split_heads(x @ Wk + bk)
        v = split_heads(x @ Wv + bv)
        scores = jnp.einsum('bhqd,bhkd->bhqk', q, k) / jnp.sqrt(jnp.float32(dk))
        causal = jnp.tril(jnp.ones((n, n), dtype=bool))
        scores = jnp.where(causal[None, None], scores, -jnp.inf)
        attn = jax.nn.softmax(scores, axis=-1)
        out = jnp.einsum('bhqk,bhkd->bhqd', attn, v)
        out = out.transpose(0, 2, 1, 3).reshape(b, n, d)
        return out @ Wo + bo

    def _L0_ffn_ref(hidden_states, gate_w, w_gate, w_up, w_down, sw_gate, sw_up, sw_down):
        import jax, jax.numpy as jnp
        import numpy as np
        H = 256
        E = 16
        K = 4
        I = 176
        IS = 176 * 2
        B, S = (1, 128)
        orig_shape = hidden_states.shape
        x = hidden_states.reshape(-1, H)
        T = x.shape[0]
        logits = jnp.einsum('th,eh->te', x, gate_w)
        scores = jax.nn.softmax(logits, axis=-1)
        topk_w, topk_idx = jax.lax.top_k(scores, K)
        topk_w = topk_w / jnp.sum(topk_w, axis=-1, keepdims=True)
        combine = jnp.zeros((T, E), dtype=x.dtype)
        combine = combine.at[jnp.arange(T)[:, None], topk_idx].add(topk_w)
        g = jnp.einsum('th,ehi->tei', x, w_gate)
        u = jnp.einsum('th,ehi->tei', x, w_up)
        a = jax.nn.silu(g) * u
        a = a * combine[:, :, None]
        y = jnp.einsum('tei,eih->th', a, w_down)
        sg = x @ sw_gate
        su = x @ sw_up
        y = y + jax.nn.silu(sg) * su @ sw_down
        return y.reshape(orig_shape)
    x = L0_attn_x
    xn = _layernorm(x, axis=-1)
    x = x + _L0_attn_ref(xn, L0_attn_Wq, L0_attn_bq, L0_attn_Wk, L0_attn_bk, L0_attn_Wv, L0_attn_bv, L0_attn_Wo, L0_attn_bo) + _L0_ffn_ref(xn, L0_ffn_gate_w, L0_ffn_w_gate, L0_ffn_w_up, L0_ffn_w_down, L0_ffn_sw_gate, L0_ffn_sw_up, L0_ffn_sw_down)
    return x

_drawn_inputs = setup_inputs


def setup_inputs(seed=0):
    import zlib

    import numpy as np

    out = dict(_drawn_inputs(seed))
    spreads = {}
    factors = {'L0_attn_bq': 64.0,
     'L0_attn_bk': 64.0,
     'L0_attn_bv': 36.409,
     'L0_attn_bo': 39.848,
     'L0_ffn_gate_w': 8.0,
     'L0_ffn_w_gate': 8.0,
     'L0_ffn_w_up': 8.0,
     'L0_ffn_w_down': 7.998,
     'L0_ffn_sw_gate': 2.907,
     'L0_ffn_sw_up': 2.878,
     'L0_ffn_sw_down': 2.875,
     'L0_attn_Wq': 3.5,
     'L0_attn_Wk': 3.512,
     'L0_attn_Wv': 2.761}
    for name, (base, spread) in spreads.items():
        noise = np.random.default_rng([zlib.crc32(name.encode()), seed]).standard_normal(out[name].shape)
        drawn = base * np.exp(spread * noise) if base else spread * noise
        out[name] = jnp.asarray(drawn.astype(out[name].dtype))
    for name, factor in factors.items():
        out[name] = (out[name] * factor).astype(out[name].dtype)
    return out
```

```python
from contextlib import ExitStack

import concourse.bass as bass
from concourse import mybir

F32 = mybir.dt.float32
F16 = mybir.dt.float16
BF16 = mybir.dt.bfloat16
I32 = mybir.dt.int32
U32 = mybir.dt.uint32
ALU = mybir.AluOpType
ACT = mybir.ActivationFunctionType
AX = mybir.AxisListType
P = 128

XS = 64.0
WS = 256.0
HS = 8.0
PASSES = [(0, 0), (0, 1), (1, 0)]
Q_TERMS = [0, 0, 0, 1, 1, 2]
K_TERMS = [0, 1, 2, 0, 1, 0]
MASKED = -1e30
LN_EPS = 1e-5


def token_mixer_with_experts(nc, x, wq, bq, wk, bk, wv, bv, wo, bo,
                             gate_w, w_gate, w_up, w_down, sw_gate, sw_up, sw_down, out):
    B, N, D = x.shape
    T = B * N
    E, _, I = w_gate.shape
    SH = sw_gate.shape[1] // I
    EW = E + SH
    H, DK = 16, D // 16
    TOPK = 4
    HC = D // P
    IP = I // 2
    TT = T // P
    CH = 512
    NCH = T // CH
    TPC = CH // P
    HG = H // 4
    NG = B * HG
    KT = N // P
    QC = N // CH
    UT = T * TOPK // P + E
    RS = UT * P
    STK = len(Q_TERMS) * DK
    STM = STK + 3
    assert D == 256 and N % CH == 0 and I % 2 == 0 and DK == 16

    nc.disable_value_cache = True
    xf = x.rearrange("b n d -> (b n) d")

    xrow_d = nc.dram_tensor("xrow_d", (T + P, 2 * D), F16).ap()
    xcol_d = nc.dram_tensor("xcol_d", (TT, P, 4 * P), F16).ap()
    q_d = nc.dram_tensor("q_d", (3, D, T), BF16).ap()
    k_d = nc.dram_tensor("k_d", (3, D, T), BF16).ap()
    v_d = nc.dram_tensor("v_d", (T, H, 2 * DK), F32).ap()
    slot_d = nc.dram_tensor("slot_d", (RS, 2), I32).ap()
    rsum_d = nc.dram_tensor("rsum_d", (2, 4, N), F32).ap()

    keep = ExitStack()
    with keep:
        def alloc(ctx):
            def sb(name, shape, dt=F32):
                return ctx.enter_context(nc.sbuf_tensor(name, shape, dt))

            def ps(name, shape, dt=F32):
                return ctx.enter_context(nc.psum_tensor(name, shape, dt))

            def sem(name):
                return ctx.enter_context(nc.semaphore(name))
            return sb, ps, sem

        sb, _, _ = alloc(keep)
        ident16 = sb("ident16", [P, P], F16)
        identb = sb("identb", [P, P], BF16)
        ident = sb("ident", [P, P])
        gu_w = sb("gu_w", [P, EW, 2, HC, 2 * I], F16)
        dn_w = sb("dn_w", [IP, EW, 2, 2, D], F16)
        woP = sb("woP", [P, HG, D])
        maskq = sb("maskq", [P, P], BF16)
        maskk = sb("maskk", [P, P], BF16)
        logits = sb("logits", [P, TT, E])
        entry = sb("entry", [P, TT * TOPK, 2], I32)
        slot_i = sb("slot_i", [P, TT * TOPK], I32)
        tile_e = sb("tile_e", [1, UT], I32)

        s = Kernel()
        s.x, s.wq, s.bq, s.wk, s.bk, s.wv, s.bv, s.wo = x, wq, bq, wk, bk, wv, bv, wo
        s.bo, s.gate_w, s.w_gate, s.w_up, s.w_down, s.sw_gate, s.sw_up, s.sw_down = bo, gate_w, w_gate, w_up, w_down, sw_gate, sw_up, sw_down
        s.xf, s.out, s.xrow_d, s.xcol_d, s.q_d, s.k_d, s.v_d, s.slot_d = xf, out, xrow_d, xcol_d, q_d, k_d, v_d, slot_d
        s.rsum_d, s.alloc, s.ident16, s.identb, s.ident, s.gu_w, s.dn_w, s.woP = rsum_d, alloc, ident16, identb, ident, gu_w, dn_w, woP
        s.maskq, s.maskk, s.logits, s.entry, s.slot_i, s.tile_e, s.B, s.N = maskq, maskk, logits, entry, slot_i, tile_e, B, N
        s.D, s.T, s.E, s.I, s.SH, s.EW, s.H, s.DK = D, T, E, I, SH, EW, H, DK
        s.TOPK, s.HC, s.IP, s.TT, s.CH, s.NCH, s.TPC, s.HG = TOPK, HC, IP, TT, CH, NCH, TPC, HG
        s.NG, s.KT, s.QC, s.UT, s.RS, s.STK, s.STM = NG, KT, QC, UT, RS, STK, STM
        weights_and_constants(nc, s)
        normalise_and_project(nc, s)
        route(nc, s)
        attention_and_experts(nc, s)


class Kernel:
    pass


def wait_apart(eng, sem, value, passed):
    eng.wait_ge(sem, value)
    eng.sem_inc(passed, 1)


def weights_and_constants(nc, s):
    D, E, EW, I, IP, HC, HG, DK = s.D, s.E, s.EW, s.I, s.IP, s.HC, s.HG, s.DK
    with ExitStack() as ctx:
        sb, ps, sem = s.alloc(ctx)
        NB = 3
        gu = sb("gu_stage", [P, NB, HC, 2, I])
        dn = sb("dn_stage", [IP, NB, 2, D])
        const_set = sem("const_set")
        const_made = sem("const_made")
        gu_in = [sem(f"gu_in{i}") for i in range(NB)]
        hi_made = sem("hi_made")
        lo_made = sem("lo_made")
        wo_clear = sem("wo_clear")
        wo_in = sem("wo_in")
        block = ctx.enter_context(nc.Block())

        def sources(e):
            if e < E:
                g, u, d = s.w_gate[e], s.w_up[e], s.w_down[e]
            else:
                c = slice((e - E) * I, (e - E + 1) * I)
                g, u, d = s.sw_gate[:, c], s.sw_up[:, c], s.sw_down[c, :]
            return (g.rearrange("(c p) i -> p c i", p=P), u.rearrange("(c p) i -> p c i", p=P),
                    d.rearrange("(c p) n -> p c n", p=IP))

        @block.sync
        def _(sp):
            for e in range(EW):
                n = e % NB
                if e >= NB:
                    sp.wait_ge(lo_made, 2 * (e - NB + 1))
                g, u, d = sources(e)
                sp.dma_start(gu[:, n, :, 0, :], g).then_inc(gu_in[n], 16)
                sp.dma_start(gu[:, n, :, 1, :], u).then_inc(gu_in[n], 16)
                sp.dma_start(dn[:, n], d).then_inc(gu_in[n], 16)

        @block.gpsimd
        def _(pool):
            pool.memset(s.woP[:, :, :], 0.0).then_inc(wo_clear, 1)
            for t in (s.ident16, s.identb, s.ident, s.maskq, s.maskk):
                last = pool.memset(t[:, :], 0.0)
            last.then_inc(const_set, 1)
            pool.wait_ge(const_set, 1)
            for t in (s.ident16, s.identb, s.ident):
                pool.affine_select(out=t[:, :], in_=t[:, :], compare_op=ALU.not_equal, fill=1.0, base=0,
                                   pattern=[[-1, P]], channel_multiplier=1)
            pool.affine_select(out=s.maskq[:, :], in_=s.maskq[:, :], compare_op=ALU.is_ge, fill=MASKED, base=0,
                               pattern=[[-1, P]], channel_multiplier=1)
            pool.affine_select(out=s.maskk[:, :], in_=s.maskk[:, :], compare_op=ALU.is_ge, fill=MASKED, base=0,
                               pattern=[[1, P]], channel_multiplier=-1).then_inc(const_made, 1)
            pool.wait_ge(wo_clear, 1)
            for hg in range(HG):
                for h in range(4):
                    r = (4 * hg + h) * DK
                    pool.dma_start(s.woP[32 * h:32 * h + DK, hg, :], s.wo[r:r + DK, :]).then_inc(wo_in, 16)
            pool.dma_start(s.woP[DK:DK + 1, 0, :], s.bo.rearrange("(a n) -> a n", a=1)).then_inc(wo_in, 16)
            pool.wait_ge(wo_in, 16 * (4 * HG + 1))
            pool.wait_ge(const_made, 1)

        @block.scalar
        def _(act):
            for e in range(EW):
                n = e % NB
                act.wait_ge(gu_in[n], 48 * (e // NB + 1))
                act.activation(s.gu_w[:, e, 0].rearrange("p c (a i) -> p c a i", a=2), gu[:, n], ACT.Copy,
                               scale=WS).then_inc(hi_made, 1)
                act.activation(s.dn_w[:, e, 0], dn[:, n], ACT.Copy, scale=WS).then_inc(hi_made, 1)

        @block.vector
        def _(dve):
            for e in range(EW):
                n = e % NB
                dve.wait_ge(hi_made, 2 * e + 1)
                dve.scalar_tensor_tensor(out=s.gu_w[:, e, 1].rearrange("p c (a i) -> p c a i", a=2), in0=gu[:, n],
                                         scalar=WS, in1=s.gu_w[:, e, 0].rearrange("p c (a i) -> p c a i", a=2),
                                         op0=ALU.mult, op1=ALU.subtract).then_inc(lo_made, 1)
                dve.wait_ge(hi_made, 2 * e + 2)
                dve.scalar_tensor_tensor(out=s.dn_w[:, e, 1], in0=dn[:, n], scalar=WS, in1=s.dn_w[:, e, 0],
                                         op0=ALU.mult, op1=ALU.subtract).then_inc(lo_made, 1)


def normalise_and_project(nc, s):
    D, E, HC, H, DK, TT, TPC, CH, NCH = s.D, s.E, s.HC, s.H, s.DK, s.TT, s.TPC, s.CH, s.NCH
    MO = D // P
    with ExitStack() as ctx:
        sb, ps, sem = s.alloc(ctx)
        w32 = sb("w32", [P, 3, HC, D])
        g32 = sb("g32", [E, D])
        w16 = sb("w16", [P, 3, 2, HC, D], F16)
        gT32 = sb("gT32", [P, HC, E])
        g16 = sb("g16", [P, 2, HC, E], F16)
        bqk = sb("bqk", [P, 2, MO])
        bvb = sb("bvb", [P, D])
        X = sb("X", [P, 2, TPC, D])
        XN = sb("XN", [P, 2, TPC, D])
        XR = sb("XR", [P, 2, TPC, 2, D], F16)
        XT = sb("XT", [P, 2, TPC, 2, HC, P], F16)
        st6 = sb("st6", [P, TPC, 6])
        mv = sb("mv", [P, TPC, 2])
        rv = sb("rv", [P, TPC])
        re_ = sb("re_", [P, TPC])
        rstd = sb("rstd", [P, 2, TPC])
        nw = sb("nw", [P, 3, TPC])
        rfin = sb("rfin", [P, TPC])
        F = sb("F", [P, 4, CH])
        R1 = sb("R1", [P, 4, CH])
        F3 = sb("F3", [P, 4, 3, CH], BF16)
        V = sb("V", [P, TPC, H, 2 * DK])
        tp = [ps(f"tp{i}", [P, 2, 4 * P], F16) for i in range(2)]
        qk = [ps(f"qk{i}", [P, CH]) for i in range(2)]
        vp = [ps(f"vp{i}", [P, 2, D]) for i in range(2)]
        lg = ps("lg", [P, TPC, E])
        gt = ps("gt", [P, HC, E])

        sp_passed = sem("sp_passed"); dve_passed = sem("dve_passed")
        w_in = sem("w_in"); b_in = sem("b_in"); w_hi = sem("w_hi"); w_lo = sem("w_lo"); v_ones = sem("v_ones")
        gt_done = sem("gt_done"); gt_out = sem("gt_out")
        x_in = [sem("x_in0"), sem("x_in1")]
        stats = sem("stats"); aggr = sem("aggr"); ve_done = sem("ve_done"); rv_done = sem("rv_done"); rstd_done = sem("rstd_done")
        nw_done = sem("nw_done"); xn_done = sem("xn_done"); xhi = sem("xhi"); xlo = sem("xlo")
        turned = sem("turned"); xt_done = sem("xt_done")
        qk_done = sem("qk_done"); f_done = sem("f_done"); f1_done = sem("f1_done"); r1_done = sem("r1_done")
        f2_done = sem("f2_done"); f3_done = sem("f3_done"); v_done = sem("v_done"); v_out = sem("v_out")
        lg_done = sem("lg_done"); lg_out = sem("lg_out")
        xr_st = sem("xr_st"); xt_st = sem("xt_st"); qk_st = sem("qk_st"); v_st = sem("v_st")
        block = ctx.enter_context(nc.Block())

        def load_x(eng, p, src):
            eng.dma_start(X[:, p], src.rearrange("(j p) d -> p j d", p=P)).then_inc(x_in[p], 16)

        @block.sync
        def _(sp):
            for i, w in enumerate((s.wq, s.wk, s.wv)):
                sp.dma_start(w32[:, i], w.rearrange("(c p) n -> p c n", p=P)).then_inc(w_in, 16)
            sp.dma_start(g32[:, :], s.gate_w).then_inc(b_in, 16)
            for i, b in enumerate((s.bq, s.bk)):
                sp.dma_start(bqk[:, i, :], b.rearrange("(m p) -> p m", p=P),
                             allow_slow_non_contiguous=True).then_inc(b_in, 16)
            sp.dma_start(bvb[:, :], s.bv.rearrange("(a n) -> a n", a=1).broadcast_to([P, D])).then_inc(b_in, 16)
            with sp.Fori(0, NCH // 2) as cc:
                for p in range(2):
                    c = cc * 2 + p
                    t0 = c * CH
                    sp.wait_ge(xlo, TPC * (c + 1))
                    sp.dma_start(s.xrow_d[bass.ds(t0, CH), :].rearrange("(j p) d -> p j d", p=P),
                                 XR[:, p].rearrange("p j a d -> p j (a d)")).then_inc(xr_st, 16)
                    sp.wait_ge(xt_done, TPC * (c + 1))
                    sp.dma_start(s.xcol_d[bass.ds(c * TPC, TPC)].rearrange("j p f -> p j f"),
                                 XT[:, p].rearrange("p j a c t -> p j (a c t)")).then_inc(xt_st, 16)
                    for i, (src, dst) in enumerate(((0, s.q_d), (0, s.q_d), (1, s.k_d), (1, s.k_d))):
                        m = i % MO
                        wait_apart(sp, f3_done, 4 * c + i + 1, sp_passed)
                        sp.dma_start(dst[:, m * P:(m + 1) * P, bass.ds(t0, CH)].rearrange("a p t -> p a t"),
                                     F3[:, i]).then_inc(qk_st, 16)
                    wait_apart(sp, v_out, 2 * c + 2, sp_passed)
                    sp.dma_start(s.v_d[bass.ds(t0, CH)].rearrange("(j p) h e -> p j (h e)", p=P),
                                 V[:, :].rearrange("p j h e -> p j (h e)")).then_inc(v_st, 16)
            sp.wait_ge(xr_st, 16 * NCH)
            sp.wait_ge(xt_st, 16 * NCH)
            sp.wait_ge(qk_st, 64 * NCH)
            sp.wait_ge(v_st, 16 * NCH)

        @block.gpsimd
        def _(pool):
            load_x(pool, 0, s.xf[0:CH, :])
            load_x(pool, 1, s.xf[CH:2 * CH, :])
            pool.memset(V[:, :, :, DK:2 * DK], 1.0).then_inc(v_ones, 1)
            with pool.Fori(0, NCH // 2 - 1) as cc:
                for p in range(2):
                    c = cc * 2 + p
                    pool.wait_ge(xn_done, TPC * (c + 1))
                    load_x(pool, p, s.xf[bass.ds((c + 2) * CH, CH), :])

        @block.scalar
        def _(act):
            act.wait_ge(w_in, 48)
            for i in range(3):
                act.activation(w16[:, i, 0], w32[:, i], ACT.Copy, scale=WS).then_inc(w_hi, 1)
            act.wait_ge(gt_out, 1)
            act.activation(g16[:, 0], gT32[:, :, :], ACT.Copy, scale=WS).then_inc(w_hi, 1)
            act.wait_ge(b_in, 64)
            with act.Fori(0, NCH // 2) as cc:
                for p in range(2):
                    c = cc * 2 + p
                    act.wait_ge(rv_done, c + 1)
                    act.activation(rstd[:, p], rv[:, :], ACT.Sqrt, scale=XS * XS).then_inc(rstd_done, 1)
                    for j in range(TPC):
                        act.wait_ge(xn_done, TPC * c + j + 1)
                        if j == 0:
                            act.wait_ge(xr_st, cc * 32)
                        act.activation(XR[:, p, j, 0], XN[:, p, j], ACT.Copy).then_inc(xhi, 1)
                    for j in range(TPC):
                        if j % 2 == 0:
                            act.wait_ge(turned, TPC * c + j + 2)
                        if j == 0:
                            act.wait_ge(xt_st, cc * 32)
                            act.wait_ge(v_done, cc * 4)
                        act.activation(XT[:, p, j].rearrange("p a c t -> p (a c t)"), tp[j // 2][:, j % 2],
                                       ACT.Copy).then_inc(xt_done, 1)
                    for i in range(4):
                        act.wait_ge(qk_done, 4 * c + i + 1)
                        if i == 0:
                            act.wait_ge(f3_done, 4 * c)
                        act.activation(F[:, i], qk[i % 2][:, :], ACT.Identity, scale=1.0 / (XS * WS),
                                       bias=bqk[:, i // 2, i % MO:i % MO + 1]).then_inc(f_done, 1)
                        act.wait_ge(f_done, 4 * c + i + 1)
                        act.wait_ge(qk_st, 64 * c)
                        act.activation(F3[:, i, 0], F[:, i], ACT.Copy).then_inc(f1_done, 1)
                        act.wait_ge(r1_done, 4 * c + i + 1)
                        act.activation(F3[:, i, 1], R1[:, i], ACT.Copy).then_inc(f2_done, 1)
                    act.wait_ge(lg_done, c + 1)
                    act.activation(s.logits[:, bass.ds(c * TPC, TPC), :], lg[:, :, :], ACT.Copy,
                                   scale=1.0 / (XS * WS)).then_inc(lg_out, 1)

        @block.vector
        def _(dve):
            def newton(c, i, ins):
                ins.then_inc(nw_done, 1)
                dve.wait_ge(nw_done, 4 * c + i + 1)

            dve.wait_ge(gt_done, 1)
            dve.tensor_copy(gT32[:, :, :], gt[:, :, :]).then_inc(gt_out, 1)
            for i in range(3):
                dve.wait_ge(w_hi, i + 1)
                dve.scalar_tensor_tensor(out=w16[:, i, 1], in0=w32[:, i], scalar=WS, in1=w16[:, i, 0],
                                         op0=ALU.mult, op1=ALU.subtract).then_inc(w_lo, 1)
            dve.wait_ge(w_hi, 4)
            dve.scalar_tensor_tensor(out=g16[:, 1], in0=gT32[:, :, :], scalar=WS, in1=g16[:, 0],
                                     op0=ALU.mult, op1=ALU.subtract).then_inc(w_lo, 1)
            dve.wait_ge(b_in, 64)
            dve.wait_ge(v_ones, 1)
            with dve.Fori(0, NCH // 2) as cc:
                for p in range(2):
                    c = cc * 2 + p
                    dve.wait_ge(x_in[p], (cc + 1) * 16)
                    for j in range(TPC):
                        dve.bn_stats(st6[:, j], X[:, p, j]).then_inc(stats, 1)
                    for j in range(TPC):
                        wait_apart(dve, stats, TPC * c + j + 1, dve_passed)
                        dve.bn_aggr(mv[:, j], st6[:, j]).then_inc(aggr, 1)
                    dve.wait_ge(aggr, TPC * (c + 1))
                    dve.tensor_scalar(re_[:, :], mv[:, :, 1], LN_EPS, None, ALU.add).then_inc(ve_done, 1)
                    dve.wait_ge(ve_done, c + 1)
                    dve.reciprocal(rv[:, :], re_[:, :]).then_inc(rv_done, 1)
                    dve.wait_ge(rstd_done, c + 1)
                    newton(c, 0, dve.tensor_tensor(nw[:, 0], rstd[:, p], rstd[:, p], ALU.mult))
                    newton(c, 1, dve.tensor_tensor(nw[:, 1], nw[:, 0], re_[:, :], ALU.mult))
                    newton(c, 2, dve.tensor_scalar(nw[:, 2], nw[:, 1], -0.5 / (XS * XS), 1.5, ALU.mult, ALU.add))
                    newton(c, 3, dve.tensor_tensor(rfin[:, :], rstd[:, p], nw[:, 2], ALU.mult))
                    for j in range(TPC):
                        dve.tensor_scalar(XN[:, p, j], X[:, p, j], mv[:, j, 0:1], rfin[:, j:j + 1],
                                          ALU.subtract, ALU.mult).then_inc(xn_done, 1)
                    for j in range(TPC):
                        dve.wait_ge(xhi, TPC * c + j + 1)
                        dve.tensor_tensor(XR[:, p, j, 1], XN[:, p, j], XR[:, p, j, 0], ALU.subtract).then_inc(xlo, 1)
                    for i in range(4):
                        dve.wait_ge(f1_done, 4 * c + i + 1)
                        dve.tensor_tensor(R1[:, i], F[:, i], F3[:, i, 0], ALU.subtract).then_inc(r1_done, 1)
                        dve.wait_ge(f2_done, 4 * c + i + 1)
                        dve.tensor_tensor(F3[:, i, 2], R1[:, i], F3[:, i, 1], ALU.subtract).then_inc(f3_done, 1)
                    for i in range(2):
                        dve.wait_ge(v_done, 2 * c + i + 1)
                        if i == 0:
                            dve.wait_ge(v_st, 16 * c)
                        dve.scalar_tensor_tensor(
                            out=V[:, 2 * i:2 * i + 2, :, 0:DK],
                            in0=vp[i][:, :, :].rearrange("p j (h e) -> p j h e", h=H), scalar=1.0 / (XS * WS),
                            in1=bvb[:, :].rearrange("p (a h e) -> p a h e", a=1, h=H).broadcast_to([P, 2, H, DK]),
                            op0=ALU.mult, op1=ALU.add).then_inc(v_out, 1)

        @block.tensor
        def _(pe):
            pe.wait_ge(b_in, 64)
            for c in range(HC):
                last = pe.transpose(gt[:, c], g32[:, c * P:(c + 1) * P], s.ident[0:E, 0:E])
            last.then_inc(gt_done, 1)
            pe.wait_ge(w_lo, 4)
            with pe.Fori(0, NCH // 2) as cc:
                for p in range(2):
                    c = cc * 2 + p
                    for j in range(TPC):
                        pe.wait_ge(xlo, TPC * c + j + 1)
                        if j % 2 == 0:
                            pe.wait_ge(xt_done, TPC * c)
                        for a in range(2):
                            for h in range(HC):
                                o = (a * HC + h) * P
                                last = pe.transpose(tp[j // 2][:, j % 2, o:o + P],
                                                    XR[:, p, j, a, h * P:(h + 1) * P], s.ident16[:, :])
                        last.then_inc(turned, 1)
                    pe.wait_ge(xt_done, TPC * (c + 1))
                    pe.wait_ge(lg_out, c)
                    for j in range(TPC):
                        terms = [(a, b, h) for a in range(2) for b in range(2) for h in range(HC)]
                        for n, (a, b, h) in enumerate(terms):
                            last = pe.matmul(lg[:, j], XT[:, p, j, a, h], g16[:, b, h], start=n == 0,
                                             stop=n == len(terms) - 1)
                    last.then_inc(lg_done, 1)
                    for i in range(4):
                        w, m = i // MO, i % MO
                        pe.wait_ge(f_done, 4 * c if i < 2 else 4 * c + i - 1)
                        n = 0
                        for a, b in PASSES:
                            for h in range(HC):
                                last = pe.matmul(qk[i % 2][:, :], w16[:, w, a, h, m * P:(m + 1) * P],
                                                 XT[:, p, :, b, h], start=n == 0, stop=n == 2 * 3 - 1)
                                n += 1
                        last.then_inc(qk_done, 1)
                    for i in range(2):
                        pe.wait_ge(v_out, 2 * c)
                        for j in range(2):
                            n = 0
                            for a, b in PASSES:
                                for h in range(HC):
                                    last = pe.matmul(vp[i][:, j], XT[:, p, 2 * i + j, a, h], w16[:, 2, b, h],
                                                     start=n == 0, stop=n == 2 * 3 - 1)
                                    n += 1
                        last.then_inc(v_done, 1)


def route(nc, s):
    TT, E, TOPK, UT, RS = s.TT, s.E, s.TOPK, s.UT, s.RS
    with ExitStack() as ctx:
        sb, ps, sem = s.alloc(ctx)
        mx = sb("mx", [P, TT])
        sh = sb("sh", [P, TT, E])
        ex = sb("ex", [P, TT, E])
        sm = sb("sm", [P, TT])
        rs = sb("rs", [P, TT])
        sc = sb("sc", [P, TT, E])
        top8 = sb("top8", [P, TT, 8])
        idx8 = sb("idx8", [P, TT, 8], U32)
        idxf = sb("idxf", [P, TT, TOPK])
        iota_e = sb("iota_e", [P, E])
        hot = sb("hot", [P, TOPK, TT, E])
        m2 = sb("m2", [P, 2, TT, E])
        chosen = sb("chosen", [P, TT, E], F16)
        tsum = sb("tsum", [P, TT])
        trec = sb("trec", [P, TT])
        tri = sb("tri", [P, P], F16)
        ones = sb("ones", [P, P], F16)
        zero = sb("zero", [P, TT])
        csum = sb("csum", [P, E, TT])
        exc = sb("exc", [P, E, TT])
        total_i = sb("total_i", [P, E], I32)
        tiles_i = sb("tiles_i", [P, E], I32)
        tiles_f = sb("tiles_f", [P, E])
        tend = sb("tend", [P, E])
        base = sb("base", [P, E])
        place = sb("place", [P, TT, E])
        pk = sb("pk", [P, TT, E])
        posf = sb("posf", [P, TT, TOPK])
        hi_i = sb("hi_i", [P, TT * TOPK], I32)
        hi_f = sb("hi_f", [P, TT * TOPK])
        pt_f = sb("pt_f", [P, TT * TOPK])
        slot_f = sb("slot_f", [P, TT * TOPK])
        iota_u = sb("iota_u", [1, UT])
        cmp = sb("cmp", [1, UT, E])
        te = sb("te", [1, UT])
        zslot = sb("zslot", [P, RS // P, 2], I32)
        zrow = sb("zrow", [P, 2 * s.D], F16)
        pos_i = sb("pos_i", [P, TT * TOPK], I32)
        rank_p = ps("rank_p", [P, TT, E])
        cnt_p = ps("cnt_p", [P, TT, E])
        const = sem("r_const"); step = sem("r_step"); expd = sem("r_exp"); mm = sem("r_mm")
        routed = sem("routed"); zeroed = sem("zeroed"); c0 = sem("r_c0")
        block = ctx.enter_context(nc.Block())

        def per_token(t):
            return t[:, :].rearrange("p (t a) -> p t a", a=1).broadcast_to([P, TT, E])

        @block.gpsimd
        def _(pool):
            pool.memset(zslot[:, :, :], 0).then_inc(c0, 1)
            pool.memset(zrow[:, :], 0.0)
            pool.memset(ones[:, :], 1.0)
            pool.memset(zero[:, :], 0.0)
            pool.iota(iota_e[:, :], [[1, E]], base=0, channel_multiplier=0, allow_small_or_imprecise_dtypes=True)
            pool.iota(iota_u[:, :], [[1, UT]], base=0, channel_multiplier=0,
                      allow_small_or_imprecise_dtypes=True).then_inc(c0, 1)
            pool.wait_ge(c0, 2)
            pool.iota(zslot[:, :, 0], [[0, UT]], base=s.T, channel_multiplier=1)
            pool.iota(s.entry[:, :, 0], [[P, TT], [0, TOPK]], base=0, channel_multiplier=1).then_inc(c0, 1)
            pool.wait_ge(c0, 3)
            pool.dma_start(s.xrow_d[s.T:s.T + P, :], zrow[:, :]).then_inc(zeroed, 16)
            pool.affine_select(out=tri[:, :], in_=ones[:, :], compare_op=ALU.is_gt, fill=0.0, base=0,
                               pattern=[[1, P]], channel_multiplier=-1).then_inc(const, 1)
            pool.dma_start(s.slot_d.rearrange("(p r) a -> p (r a)", p=P),
                           zslot[:, :, :].rearrange("p r a -> p (r a)")).then_inc(zeroed, 16)
            pool.wait_ge(zeroed, 32)

        @block.scalar
        def _(act):
            act.wait_ge(step, 2)
            act.activation(ex[:, :, :], sh[:, :, :], ACT.Exp).then_inc(expd, 1)

        @block.tensor
        def _(pe):
            pe.wait_ge(const, 1)
            pe.wait_ge(mm, 1)
            pe.matmul(rank_p[:, :, :], tri[:, :], chosen[:, :, :], start=True, stop=True).then_inc(mm, 1)
            pe.matmul(cnt_p[:, :, :], ones[:, :], chosen[:, :, :], start=True, stop=True).then_inc(mm, 1)

        @block.vector
        def _(dve):
            done = [0]

            def then(ins):
                done[0] += 1
                ins.then_inc(step, 1)
                dve.wait_ge(step, done[0])

            then(dve.tensor_reduce(mx[:, :], s.logits[:, :, :], AX.X, ALU.max))
            then(dve.tensor_tensor(sh[:, :, :], s.logits[:, :, :], per_token(mx), ALU.subtract))
            dve.wait_ge(expd, 1)
            dve.wait_ge(const, 1)
            then(dve.tensor_reduce(sm[:, :], ex[:, :, :], AX.X, ALU.add))
            then(dve.reciprocal(rs[:, :], sm[:, :]))
            then(dve.tensor_tensor(sc[:, :, :], ex[:, :, :], per_token(rs), ALU.mult))
            for t in range(TT):
                last = dve.max(top8[:, t], sc[:, t])
            then(last)
            for t in range(TT):
                last = dve.max_index(idx8[:, t], top8[:, t], sc[:, t])
            then(last)
            then(dve.tensor_copy(idxf[:, :, :], idx8[:, :, 0:TOPK]))
            then(dve.tensor_reduce(tsum[:, :], top8[:, :, 0:TOPK], AX.X, ALU.add))
            then(dve.reciprocal(trec[:, :], tsum[:, :]))
            then(dve.scalar_tensor_tensor(out=s.entry[:, :, :].bitcast(F32)[:, :, 1].rearrange("p (t k) -> p t k", k=TOPK),
                                          in0=top8[:, :, 0:TOPK], scalar=1.0 / (HS * WS),
                                          in1=trec[:, :].rearrange("p (t a) -> p t a", a=1)
                                          .broadcast_to([P, TT, TOPK]), op0=ALU.mult, op1=ALU.mult))
            for k in range(TOPK):
                then(dve.tensor_tensor(hot[:, k], idxf[:, :, k:k + 1].broadcast_to([P, TT, E]),
                                       iota_e[:, :].rearrange("p (a e) -> p a e", a=1).broadcast_to([P, TT, E]),
                                       ALU.is_equal))
            then(dve.tensor_tensor(m2[:, 0], hot[:, 0], hot[:, 1], ALU.add))
            then(dve.tensor_tensor(m2[:, 1], hot[:, 2], hot[:, 3], ALU.add))
            then(dve.tensor_tensor(chosen[:, :, :], m2[:, 0], m2[:, 1], ALU.add))
            dve.tensor_copy(m2[:, 0], chosen[:, :, :]).then_inc(mm, 1)
            dve.wait_ge(mm, 3)
            for e in range(E):
                last = dve.tensor_tensor_scan(csum[:, e], cnt_p[:, :, e], zero[:, :], 0.0, ALU.add, ALU.add)
            then(last)
            then(dve.tensor_tensor(exc[:, :, :], csum[:, :, :], cnt_p[:, :, :].rearrange("p t e -> p e t"), ALU.subtract))
            then(dve.tensor_scalar(total_i[:, :], csum[:, :, TT - 1], float(P - 1), None, ALU.add))
            then(dve.tensor_scalar(tiles_i[:, :], total_i[:, :], 7, None, ALU.arith_shift_right))
            then(dve.tensor_copy(tiles_f[:, :], tiles_i[:, :]))
            then(dve.tensor_tensor_scan(tend[:, :], tiles_f[:, :], zero[:, 0:E], 0.0, ALU.add, ALU.add))
            then(dve.tensor_tensor(base[:, :], tend[:, :], tiles_f[:, :], ALU.subtract))
            then(dve.tensor_scalar(base[:, :], base[:, :], float(P), None, ALU.mult))
            then(dve.tensor_tensor(place[:, :, :], rank_p[:, :, :], exc[:, :, :].rearrange("p e t -> p t e"), ALU.add))
            then(dve.tensor_tensor(place[:, :, :], place[:, :, :],
                                   base[:, :].rearrange("p (a e) -> p a e", a=1).broadcast_to([P, TT, E]), ALU.add))
            for k in range(TOPK):
                then(dve.tensor_tensor(pk[:, :, :], place[:, :, :], hot[:, k], ALU.mult))
                then(dve.tensor_reduce(posf[:, :, k], pk[:, :, :], AX.X, ALU.add))
            pf = posf[:, :, :].rearrange("p t k -> p (t k)")
            then(dve.tensor_copy(pos_i[:, :], pf))
            then(dve.tensor_scalar(hi_i[:, :], pos_i[:, :], 7, None, ALU.arith_shift_right))
            then(dve.tensor_copy(hi_f[:, :], hi_i[:, :]))
            then(dve.tensor_scalar(pt_f[:, :], pf, float(UT), None, ALU.mult))
            then(dve.scalar_tensor_tensor(out=slot_f[:, :], in0=hi_f[:, :], scalar=1.0 - P * UT, in1=pt_f[:, :],
                                          op0=ALU.mult, op1=ALU.add))
            then(dve.tensor_copy(s.slot_i[:, :], slot_f[:, :]))
            then(dve.tensor_tensor(cmp[:, :, 0:E - 1],
                                   iota_u[:, :].rearrange("p (u a) -> p u a", a=1).broadcast_to([1, UT, E - 1]),
                                   tend[0:1, 0:E - 1].rearrange("p (a e) -> p a e", a=1).broadcast_to([1, UT, E - 1]),
                                   ALU.is_ge))
            then(dve.tensor_reduce(te[:, :], cmp[:, :, 0:E - 1], AX.X, ALU.add))
            dve.tensor_copy(s.tile_e[:, :], te[:, :]).then_inc(routed, 1)


def attention_and_experts(nc, s):
    D, N, B, H, DK, HG, NG, KT, QC, CH, TT = s.D, s.N, s.B, s.H, s.DK, s.HG, s.NG, s.KT, s.QC, s.CH, s.TT
    STK, STM = s.STK, s.STM
    E, SH, I, IP, HC, UT, TOPK, T = s.E, s.SH, s.I, s.IP, s.HC, s.UT, s.TOPK, s.T
    with ExitStack() as ctx:
        sb, ps, sem = s.alloc(ctx)
        Qs = sb("Qs", [STM, 2, 4, N], BF16)
        Ks = sb("Ks", [STM, 2, 4, N], BF16)
        Vs = sb("Vs", [P, 2, KT, 4, 2 * DK])
        PB = 3
        probs = sb("probs", [P, PB, 4 * CH])
        part = sb("part", [P, 2, 2, 4, KT])
        rmax = sb("rmax", [P, 2, 4 * KT])
        nm = sb("nm", [4 * KT, 2, 3, P], BF16)
        nres = sb("nres", [4 * KT, P])
        oe = sb("oe", [P, QC, CH])
        sums = sb("sums", [P, 4 * N // P])
        recs = sb("recs", [P, 4 * N // P])
        rb = sb("rb", [P, QC, CH])
        OT = sb("OT", [P, HG, N])
        YA = sb("YA", [P, 2, D])
        slots = sb("slots", [P, UT, 2], I32)
        GB, AHEAD = 6, 4
        idx = sb("idx", [P, GB], I32)
        XG = sb("XG", [P, GB, 2, HC, P], F16)
        XC = sb("XC", [P, 2, 2, HC, P], F16)
        xs = sb("xs", [P, 2, D])
        nothing = sb("nothing", [P, D])
        th = sb("th", [P, I])
        sg = sb("sg", [P, I])
        hf = sb("hf", [P, I])
        h16 = sb("h16", [IP, 2, 2, 2, P], F16)
        Y = sb("Y", [P, 2, D])
        smp = [ps(f"smp{i}", [P, CH]) for i in range(2)]
        stp = [ps(f"stp{i}", [P, CH]) for i in range(2)]
        pvp = ps("pvp", [P, CH])
        gup = ps("gup", [P, CH])
        turn = ps("turn", [P, CH])
        outs = ps("outs", [P, 2, D])
        xp = turn[:, 0:2 * P].bitcast(F16)
        hp = turn[0:IP, 0:2 * P]
        mxp = turn[0:4 * KT, 2 * P:3 * P]
        yp = outs[:, 0]
        wop = outs[:, 1]

        PIECES = 38
        SU = TT * SH
        NV = SU + UT
        B0U = SU // HG
        BU = UT // (NG - HG)

        def max_pieces():
            out = []
            for t in range(KT):
                for k0 in range(0, (t + 1) * P, CH):
                    w = min(CH, (t + 1) * P - k0)
                    n = CH // w if w in (128, 256, 512) else 1
                    for h in range(0, 4, n):
                        out.append((t, k0, w, h, n))
            assert len(out) == PIECES
            return out

        def key_steps():
            return [(q, t, max(0, t * P - q * CH)) for q in range(QC) for t in range((q + 1) * CH // P)]

        def score_pieces():
            out = []
            for n, (q, t, q0) in enumerate(key_steps()):
                w = CH - q0
                m = CH // w if w in (128, 256, 512) else 1
                for h in range(0, 4, m):
                    out.append((n, h, m))
            assert len(out) == PIECES
            return out

        MAXP, STEPS, SCP = max_pieces(), key_steps(), score_pieces()
        NST = len(STEPS)
        MAX_FROM, MAX_TO = 4, 30
        TURN = 31
        RECIPS, FINISH, OUT0 = 4, 10, 12
        RT = HG * BU
        ADDS = RT + KT

        def next_pieces(n):
            a = (n - MAX_FROM) * PIECES // (MAX_TO - MAX_FROM)
            z = (n - MAX_FROM + 1) * PIECES // (MAX_TO - MAX_FROM)
            return range(max(0, min(a, PIECES)), max(0, min(z, PIECES)))

        def units_at(n, many):
            return [j for j in range(many) if j * (PIECES - 2) // many == n]

        def tiles_at(n):
            return [t for t in range(KT) if 14 + 3 * t == n]

        def added_before(b, k):
            return 1 + (b - 1) * ADDS + k + max(0, min(KT, k - 5))

        qk_in = [sem("qk_in0"), sem("qk_in1")]
        v_in = [sem("v_in0"), sem("v_in1")]
        a_const = sem("a_const"); a_ones = sem("a_ones")
        smax_done = sem("smax_done"); red_done = sem("red_done"); rmax_done = sem("rmax_done")
        mT_done = sem("mT_done"); nm_a = sem("nm_a"); nm_done = sem("nm_done"); nm_in = sem("nm_in")
        st_done = sem("st_done"); exp_done = sem("exp_done"); pv_done = sem("pv_done"); oe_done = sem("oe_done")
        sums_in = sem("sums_in"); rec_done = sem("rec_done"); rec_st = sem("rec_st"); rb_in = sem("rb_in")
        ot_done = sem("ot_done"); wo_done = sem("wo_done"); ya_done = sem("ya_done")
        scattered = sem("scattered"); sl_in = sem("sl_in"); idx_done = sem("idx_done")
        xg_in = [sem(f"xg_in{i}") for i in range(GB)]
        xc_in = [sem("xc_in0"), sem("xc_in1")]; xs_in = [sem("xs_in0"), sem("xs_in1")]
        xp_done = sem("xp_done"); xc_done = sem("xc_done"); gu_done = sem("gu_done"); th_done = sem("th_done")
        sg_done = sem("sg_done"); hf_done = sem("hf_done"); hT_done = sem("hT_done"); hh_done = sem("hh_done"); hl_done = sem("hl_done")
        y_done = sem("y_done"); yo_done = sem("yo_done"); out_st = [sem("out_st0"), sem("out_st1")]; added = sem("added")
        block = ctx.enter_context(nc.Block())

        def over_batches(batch):
            for b in range(B):
                batch(b, b == 0, b == B - 1)

        @block.gpsimd
        def _(pool):
            for b in range(2):
                pool.memset(part[:, b, 1], -3.0e38)
            pool.memset(nothing[:, :], 0.0).then_inc(a_const, 1)
            pool.wait_ge(a_const, 1)
            pool.dma_start(s.out[T:T + P, :], nothing[:, :]).then_inc(added, 16)
            for i in range(TT * TOPK):
                pool.indirect_dma_start(s.slot_d, bass.IndirectOffsetOnAxis(ap=s.slot_i[:, i:i + 1], axis=0),
                                        s.entry[:, i, :], None).then_inc(scattered, 16)
            pool.wait_ge(scattered, 16 * TT * TOPK)
            pool.dma_start(slots[:, :, :].rearrange("p u a -> p (u a)"),
                           s.slot_d.rearrange("(p u) a -> p (u a)", p=P)).then_inc(sl_in, 16)
            pool.wait_ge(sl_in, 16)

            def gather(r, q):
                pool.tensor_copy(idx[:, q:q + 1], slots[:, r, 0:1]).then_inc(idx_done, 1)
                pool.wait_ge(idx_done, r + 1)
                pool.indirect_dma_start(XG[:, q].rearrange("p a c t -> p (a c t)"), None, s.xrow_d,
                                        bass.IndirectOffsetOnAxis(ap=idx[:, q:q + 1], axis=0)).then_inc(xg_in[q], 16)

            def scatter_add(b, k, r):
                pool.wait_ge(yo_done, r + TT + 1)
                pool.wait_ge(added, 16 * added_before(b, k))
                pool.indirect_dma_start(s.out, bass.IndirectOffsetOnAxis(ap=idx[:, k % GB:k % GB + 1], axis=0),
                                        Y[:, k % 2], None, compute_op=ALU.add).then_inc(added, 16)

            def add_attention(tile, t, adds):
                pool.wait_ge(ya_done, tile + 1)
                pool.wait_ge(added, 16 * adds)
                pool.dma_start(s.out[tile * P:(tile + 1) * P, :], YA[:, t % 2], accum_op=ALU.add).then_inc(added, 16)

            for r in range(AHEAD):
                gather(r, r % GB)
            for i in range(2):
                pool.wait_ge(out_st[i], 16 * TT // 2)

            def batch(b, last):
                for k in range(RT):
                    r = (b - 1) * RT + k
                    if not last or k + AHEAD < RT:
                        gather(r + AHEAD, (k + AHEAD) % GB)
                    scatter_add(b, k, r)
                    t = k - 5
                    if 0 <= t < KT:
                        add_attention((b - 1) * KT + t, t, added_before(b, k) + 1)

            for b in range(1, B):
                batch(b, b == B - 1)
            for t in range(KT):
                tile = (B - 1) * KT + t
                add_attention(tile, t, 1 + UT + tile)
            pool.wait_ge(added, 16 * (1 + UT + TT))

        @block.sync
        def _(sp):
            def load_group(b, hg, p):
                t0 = b * N
                for dst, src, terms in ((Ks, s.k_d, K_TERMS), (Qs, s.q_d, Q_TERMS)):
                    for n, a in enumerate(terms):
                        sp.dma_start(dst[n * DK:(n + 1) * DK, p],
                                     src[a, hg * 4 * DK:(hg + 1) * 4 * DK, t0:t0 + N]
                                     .rearrange("(h r) t -> r h t", h=4)).then_inc(qk_in[p], 16)
                sp.dma_start(Vs[:, p].rearrange("p k h e -> p k (h e)"),
                             s.v_d[t0:t0 + N, 4 * hg:4 * hg + 4, :]
                             .rearrange("(k p) h e -> p k (h e)", p=P)).then_inc(v_in[p], 16)

            def send_max(g, p):
                sp.wait_ge(nm_done, g + 1)
                for a in range(3):
                    sp.dma_start(Qs[STK + a:STK + a + 1, p].rearrange("o h (t q) -> o (h t) q", q=P),
                                 nm[:, p, a, :]).then_inc(nm_in, 16)

            def send_sums(g, q2):
                sp.wait_ge(oe_done, QC * (g + 1))
                for h in range(4):
                    sp.dma_start(sums[32 * h:32 * h + 32, :],
                                 oe[32 * h + DK:32 * h + DK + 1].rearrange("o q (p c) -> o (q p) c", p=32 // QC))\
                        .then_inc(sums_in, 16)
                sp.wait_ge(rec_done, g + 1)
                sp.dma_start(s.rsum_d[q2].rearrange("h (p c) -> (h p) c", p=32), recs[:, :]).then_inc(rec_st, 16)
                sp.wait_ge(rec_st, 16 * (g + 1))
                for h in range(4):
                    sp.dma_start(rb[32 * h:32 * h + 32].rearrange("p q c -> p (q c)"),
                                 s.rsum_d[q2, h:h + 1, :].broadcast_to([32, N])).then_inc(rb_in, 16)

            def shared_columns(t):
                if t >= 2:
                    sp.wait_ge(gu_done, SH * (t - 1))
                sp.dma_start(XC[:, t % 2].rearrange("p a c t -> p (a c t)"), s.xcol_d[t]).then_inc(xc_in[t % 2], 16)

            def shared_rows(t):
                if t >= 2:
                    sp.wait_ge(yo_done, t - 1)
                sp.dma_start(xs[:, t % 2], s.xf[t * P:(t + 1) * P, :]).then_inc(xs_in[t % 2], 16)

            def store_shared(t):
                sp.wait_ge(yo_done, t + 1)
                sp.dma_start(s.out[t * P:(t + 1) * P, :], Y[:, t % 2]).then_inc(out_st[t % 2], 16)

            def shared_tiles(begin, end):
                for t in range(max(0, begin), end):
                    if t + 2 < TT:
                        shared_columns(t + 2)
                    store_shared(t)
                    if t + 2 < TT:
                        shared_rows(t + 2)

            def batch(b, first, last):
                for hg in range(HG):
                    g = b * HG + hg
                    p = hg % 2
                    if not (last and hg == HG - 1):
                        if g:
                            sp.wait_ge(pv_done, NST * g)
                        load_group(b if hg < HG - 1 else b + 1, (hg + 1) % HG, 1 - p)
                    if first and hg:
                        shared_tiles(hg * (B0U // SH) - 1, hg * (B0U // SH))
                    if not (first and hg == 0):
                        send_sums(g - 1, 1 - p)
                    if first:
                        shared_tiles(hg * (B0U // SH), (hg + 1) * (B0U // SH) - 1)
                    if not (last and hg == HG - 1):
                        send_max(g + 1, 1 - p)
                if first:
                    shared_tiles(TT - 1, TT)

            load_group(0, 0, 0)
            for t in range(2):
                shared_columns(t)
                shared_rows(t)
            send_max(0, 0)
            over_batches(batch)
            send_sums(NG - 1, 1)
            for i in range(2):
                sp.wait_ge(out_st[i], 16 * TT // 2)

        @block.tensor
        def _(pe):
            def max_piece(g, p, r, n):
                t, k0, w, h0, nh = MAXP[n]
                bank = smp[n % 2]
                if n == 0:
                    pe.wait_ge(qk_in[p], 16 * 12 * (r + 1))
                if PIECES * g + n >= 2:
                    pe.wait_ge(red_done, PIECES * g + n - 1)
                for i in range(nh):
                    h = h0 + i
                    diag = k0 + w == (t + 1) * P
                    last = pe.matmul(bank[:, i * w:(i + 1) * w], Qs[0:STK, p, h, t * P:(t + 1) * P],
                                     Ks[0:STK, p, h, k0:k0 + w], start=True, stop=not diag)
                    if diag:
                        last = pe.matmul(bank[:, (i + 1) * w - P:(i + 1) * w], s.identb[:, :], s.maskq[:, :],
                                         start=False, stop=True)
                last.then_inc(smax_done, 1)

            def turn_max(g, p, turned, units):
                pe.wait_ge(rmax_done, g + 1)
                if turned:
                    pe.wait_ge(xc_done, turned)
                if units:
                    pe.wait_ge(hl_done, units)
                pe.transpose(mxp, rmax[:, p, :], s.ident[:, :]).then_inc(mT_done, 1)

            def score_piece(g, p, n):
                st, h0, nh = SCP[n]
                q, t, q0 = STEPS[st]
                w = CH - q0
                bank = stp[n % 2]
                if n == 0:
                    pe.wait_ge(nm_in, 48 * (g + 1))
                if PIECES * g + n >= 2:
                    pe.wait_ge(exp_done, PIECES * g + n - 1)
                for i in range(nh):
                    h = h0 + i
                    diag = t * P >= q * CH
                    last = pe.matmul(bank[:, i * w:(i + 1) * w], Ks[:, p, h, t * P:(t + 1) * P],
                                     Qs[:, p, h, q * CH + q0:(q + 1) * CH], start=True, stop=not diag)
                    if diag:
                        last = pe.matmul(bank[:, i * w:i * w + P], s.identb[:, :], s.maskk[:, :],
                                         start=False, stop=True)
                last.then_inc(st_done, 1)

            def values(g, p, r, st):
                q, t, q0 = STEPS[st]
                w = CH - q0
                if st == 0:
                    pe.wait_ge(v_in[p], 16 * (r + 1))
                if t == 0 and g + q:
                    pe.wait_ge(oe_done, QC * g + q)
                lastp = max(n for n, x in enumerate(SCP) if x[0] == st)
                pe.wait_ge(exp_done, PIECES * g + lastp + 1)
                for h in range(4):
                    last = pe.matmul(pvp[32 * h:32 * h + 32, q0:CH], Vs[:, p, t, h, :],
                                     probs[:, st % PB, h * w:(h + 1) * w], start=t == 0,
                                     stop=t == (q + 1) * CH // P - 1, tile_position=(0, 32 * h))
                last.then_inc(pv_done, 1)

            def project(tile, t, normal, youts):
                if t == 0:
                    pe.wait_ge(ot_done, normal)
                if tile:
                    pe.wait_ge(ya_done, tile)
                pe.wait_ge(yo_done, youts)
                for hg in range(HG):
                    last = pe.matmul(wop, OT[:, hg, t * P:(t + 1) * P], s.woP[:, hg, :],
                                     start=hg == 0, stop=hg == HG - 1)
                last.then_inc(wo_done, 1)

            def turn_rows(b, k, maxima, units):
                r = (b - 1) * RT + k
                q = k % GB
                pe.wait_ge(xg_in[q], 16 * ((b - 1) * (RT // GB) + k // GB + 1))
                if r:
                    pe.wait_ge(xc_done, r)
                pe.wait_ge(nm_done, maxima)
                pe.wait_ge(hl_done, units)
                for a in range(2):
                    for h in range(HC):
                        o = (a * HC + h) * P
                        last = pe.transpose(xp[:, o:o + P], XG[:, q, a, h], s.ident16[:, :])
                last.then_inc(xp_done, 1)

            def expert_of(r):
                return pe.value_load(s.tile_e[0:1, r:r + 1], min_val=0, max_val=E - 1)

            def weights_of(t, e, *ix):
                if isinstance(e, int):
                    return t[(slice(None), e) + ix]
                return t[(slice(None), bass.ds(e, 1)) + ix].rearrange("p o i -> p (o i)")

            def gate_up(v, xb, e):
                if v:
                    pe.wait_ge(hf_done, v)
                n = 0
                for a, b in PASSES:
                    for h in range(HC):
                        last = pe.matmul(gup[:, 0:2 * I], XC[:, xb, a, h], weights_of(s.gu_w, e, b, h, slice(0, 2 * I)),
                                         start=n == 0, stop=n == 5)
                        n += 1
                last.then_inc(gu_done, 1)

            def turn_h(v, turned, maxima):
                pe.wait_ge(hf_done, v + 1)
                if turned:
                    pe.wait_ge(xc_done, turned)
                pe.wait_ge(nm_done, maxima)
                for c in range(2):
                    last = pe.transpose(hp[:, c * P:(c + 1) * P], hf[:, c * IP:(c + 1) * IP], s.ident[:, :])
                last.then_inc(hT_done, 1)

            def down(v, hb, e, begin, end):
                pe.wait_ge(hl_done, v + 1)
                n = 0
                for c in range(2):
                    for a, b in PASSES:
                        last = pe.matmul(yp, h16[:, hb, a, c], weights_of(s.dn_w, e, b, c, slice(0, D)),
                                         start=begin and n == 0, stop=end and n == 5)
                        n += 1
                last.then_inc(y_done, 1)

            def shared_down(v):
                if v >= SH and v % SH == 0:
                    pe.wait_ge(yo_done, v // SH)
                down(v, v % 2, E + v % SH, v % SH == 0, v % SH == SH - 1)

            def routed_down(b, k, e, projected):
                r = (b - 1) * RT + k
                pe.wait_ge(yo_done, TT + r)
                if (b - 1) * KT + projected:
                    pe.wait_ge(ya_done, (b - 1) * KT + projected)
                down(SU + r, k % 2, e, True, True)

            def batch(b, first, last):
                projected = 0
                turned = 0
                downs = 0
                units = 0
                many = B0U if first else BU
                e_before = None
                if not first:
                    r0 = (b - 1) * RT
                    turn_rows(b, 0, b * HG + 1, SU + r0)
                    e_here = expert_of(r0)
                    turned = 1
                for hg in range(HG):
                    g = b * HG + hg
                    p = hg % 2
                    more = not (last and hg == HG - 1)
                    r = b * (HG // 2) + hg // 2
                    nst = 0
                    for n in range(PIECES):
                        here = units_at(n, B0U if first else BU)
                        maxima = g + 2 if more and n > TURN else g + 1
                        for j in here:
                            if first:
                                v = hg * B0U + j
                                if v % SH == 0:
                                    pe.wait_ge(xc_in[v // SH % 2], 16 * (v // SH // 2 + 1))
                                gate_up(v, v // SH % 2, E + v % SH)
                            else:
                                k = hg * BU + j
                                pe.wait_ge(xc_done, r0 + k + 1)
                                gate_up(SU + r0 + k, k % 2, e_here)
                        score_piece(g, p, n)
                        for j in here:
                            v = hg * B0U + j
                            k = hg * BU + j
                            if first and v:
                                shared_down(v - 1)
                            if not first and k:
                                routed_down(b, k - 1, e_before, projected)
                                downs += 1
                            if not first and k + 1 < RT:
                                turn_rows(b, k + 1, maxima, SU + r0 + units)
                                turned += 1
                        if more:
                            for m in next_pieces(n):
                                max_piece(g + 1, 1 - p, b * (HG // 2) + (hg + 1) // 2, m)
                        if not first and hg == 0:
                            for t in tiles_at(n):
                                project((b - 1) * KT + t, t, QC * g, TT + r0 + downs)
                                projected += 1
                        while nst < NST and SCP[n][0] > nst:
                            values(g, p, r, nst)
                            nst += 1
                        for j in units_at(n - 1, many):
                            if first:
                                turn_h(hg * B0U + j, 0, maxima)
                            else:
                                turn_h(SU + r0 + hg * BU + j, r0 + turned, maxima)
                                e_before = e_here
                                if hg * BU + j + 1 < RT:
                                    e_here = expert_of(r0 + hg * BU + j + 1)
                            units = hg * many + j + 1
                        if more and n == TURN:
                            turn_max(g + 1, 1 - p, 0 if first else r0 + turned, units if first else SU + r0 + units)
                    while nst < NST:
                        values(g, p, r, nst)
                        nst += 1
                if first:
                    shared_down(SU - 1)
                else:
                    routed_down(b, RT - 1, e_before, projected)

            pe.wait_ge(a_ones, 1)
            for n in range(PIECES):
                max_piece(0, 0, 0, n)
            turn_max(0, 0, 0, 0)
            over_batches(batch)
            for t in range(KT):
                project((B - 1) * KT + t, t, QC * NG, TT + UT)

        @block.vector
        def _(dve):
            def reduce_piece(g, p, n):
                t, k0, w, h0, nh = MAXP[n]
                dve.wait_ge(smax_done, PIECES * g + n + 1)
                dve.tensor_reduce(part[:, p, k0 // CH, h0:h0 + nh, t],
                                  smp[n % 2][:, 0:nh * w].rearrange("p (h k) -> p h k", h=nh), AX.X,
                                  ALU.max).then_inc(red_done, 1)

            def close_max(g, p):
                dve.wait_ge(red_done, PIECES * (g + 1))
                dve.tensor_tensor(rmax[:, p, :], part[:, p, 0].rearrange("p h t -> p (h t)"),
                                  part[:, p, 1].rearrange("p h t -> p (h t)"), ALU.max).then_inc(rmax_done, 1)
                dve.wait_ge(mT_done, g + 1)
                dve.tensor_scalar(nm[:, p, 0], mxp, -1.0, None, ALU.mult).then_inc(nm_a, 1)
                dve.wait_ge(nm_a, 3 * g + 1)
                dve.scalar_tensor_tensor(out=nres[:, :], in0=mxp, scalar=-1.0, in1=nm[:, p, 0], op0=ALU.mult,
                                         op1=ALU.subtract).then_inc(nm_a, 1)
                dve.wait_ge(nm_a, 3 * g + 2)
                dve.tensor_copy(nm[:, p, 1], nres[:, :]).then_inc(nm_a, 1)
                dve.wait_ge(nm_a, 3 * g + 3)
                dve.tensor_tensor(nm[:, p, 2], nres[:, :], nm[:, p, 1], ALU.subtract).then_inc(nm_done, 1)

            def out_chunk(g, q):
                dve.wait_ge(pv_done, NST * g + (CH // P if q == 0 else NST))
                dve.tensor_copy(oe[:, q], pvp[:, :]).then_inc(oe_done, 1)

            def reciprocals(g):
                dve.wait_ge(sums_in, 64 * (g + 1))
                dve.reciprocal(recs[:, :], sums[:, :]).then_inc(rec_done, 1)

            def normalise(g, hg):
                dve.wait_ge(rb_in, 64 * (g + 1))
                for q in range(QC):
                    dve.tensor_tensor(OT[:, hg, q * CH:(q + 1) * CH], rb[:, q], oe[:, q], ALU.mult).then_inc(ot_done, 1)

            def silu_times_up(v):
                dve.wait_ge(th_done, v + 1)
                dve.scalar_tensor_tensor(out=sg[:, :], in0=th[:, :], scalar=1.0, in1=gup[:, 0:I],
                                         op0=ALU.add, op1=ALU.mult).then_inc(sg_done, 1)
                dve.wait_ge(sg_done, v + 1)
                if v:
                    dve.wait_ge(hT_done, v)
                dve.scalar_tensor_tensor(out=hf[:, :], in0=sg[:, :], scalar=0.5 * HS / (XS * WS) ** 2,
                                         in1=gup[:, I:2 * I], op0=ALU.mult, op1=ALU.mult).then_inc(hf_done, 1)

            def low_part(v, hb):
                dve.wait_ge(hh_done, v + 1)
                dve.tensor_tensor(h16[:, hb, 1].rearrange("i c t -> i (c t)"), hp,
                                  h16[:, hb, 0].rearrange("i c t -> i (c t)"), ALU.subtract).then_inc(hl_done, 1)

            def shared_out(t):
                dve.wait_ge(y_done, SH * (t + 1))
                dve.wait_ge(xs_in[t % 2], 16 * (t // 2 + 1))
                if t >= 2:
                    dve.wait_ge(out_st[t % 2], 16 * (t // 2))
                dve.scalar_tensor_tensor(out=Y[:, t % 2], in0=yp, scalar=1.0 / (HS * WS), in1=xs[:, t % 2],
                                         op0=ALU.mult, op1=ALU.add).then_inc(yo_done, 1)

            def attention_out(tile, t, adds):
                dve.wait_ge(wo_done, tile + 1)
                dve.wait_ge(added, 16 * adds)
                dve.tensor_copy(YA[:, t % 2], wop).then_inc(ya_done, 1)

            def batch(b, first, last):
                many = B0U if first else BU
                for hg in range(HG):
                    g = b * HG + hg
                    p = hg % 2
                    more = not (last and hg == HG - 1)
                    for n in range(PIECES):
                        here = units_at(n, B0U if first else BU)
                        for j in here:
                            v = hg * B0U + j if first else SU + (b - 1) * RT + hg * BU + j
                            silu_times_up(v)
                        if more:
                            for m in next_pieces(n):
                                reduce_piece(g + 1, 1 - p, m)
                        for j in here:
                            v = hg * B0U + j
                            if first and v % SH == 0 and v:
                                shared_out(v // SH - 1)
                        for j in units_at(n - 1, many):
                            low_part(hg * B0U + j if first else SU + (b - 1) * RT + hg * BU + j, j % 2)
                        if not first and hg == 0:
                            for t in tiles_at(n):
                                attention_out((b - 1) * KT + t, t,
                                              added_before(b, 0) if t < 2 else added_before(b, t + 3) + 2)
                        if not (first and hg == 0):
                            if n == RECIPS:
                                reciprocals(g - 1)
                            if n == FINISH:
                                normalise(g - 1, (hg - 1) % HG)
                        if n == OUT0:
                            out_chunk(g, 0)
                        if more and n == TURN:
                            close_max(g + 1, 1 - p)
                    out_chunk(g, 1)
                if first:
                    shared_out(TT - 1)

            dve.memset(Ks[STK:STM], 1.0).then_inc(a_ones, 1)
            dve.wait_ge(a_const, 1)
            for n in range(PIECES):
                reduce_piece(0, 0, n)
            close_max(0, 0)
            over_batches(batch)
            reciprocals(NG - 1)
            normalise(NG - 1, HG - 1)
            for t in range(KT):
                attention_out((B - 1) * KT + t, t, 1 + UT + (B - 1) * KT + max(0, t - 1))

        @block.scalar
        def _(act):
            def exps(g, n):
                st, h0, nh = SCP[n]
                w = CH - STEPS[st][2]
                act.wait_ge(st_done, PIECES * g + n + 1)
                if h0 == 0 and NST * g + st >= PB:
                    act.wait_ge(pv_done, NST * g + st - PB + 1)
                act.activation(probs[:, st % PB, h0 * w:(h0 + nh) * w], stp[n % 2][:, 0:nh * w], ACT.Exp,
                               scale=float(DK) ** -0.5).then_inc(exp_done, 1)

            def gates(v):
                act.wait_ge(gu_done, v + 1)
                if v:
                    act.wait_ge(sg_done, v)
                act.activation(th[:, :], gup[:, 0:I], ACT.Tanh, scale=0.5 / (XS * WS)).then_inc(th_done, 1)

            def high_part(v, hb):
                act.wait_ge(hT_done, v + 1)
                if v >= 2:
                    act.wait_ge(y_done, v - 1)
                act.activation(h16[:, hb, 0].rearrange("i c t -> i (c t)"), hp, ACT.Copy).then_inc(hh_done, 1)

            def columns(r, q):
                act.wait_ge(xp_done, r + 1)
                act.wait_ge(gu_done, SU + r - 1)
                act.activation(XC[:, q].rearrange("p a c t -> p (a c t)"), xp, ACT.Copy).then_inc(xc_done, 1)

            def routed_out(b, k):
                r = (b - 1) * RT + k
                act.wait_ge(y_done, SU + r + 1)
                if k == 0:
                    act.wait_ge(sl_in, 16)
                    for i in range(2):
                        act.wait_ge(out_st[i], 16 * TT // 2)
                act.wait_ge(added, 16 * (added_before(b, 0) if k < 2 else added_before(b, k - 2) + 1))
                weight = slots[:, :, :].bitcast(F32)[:, r, 1:2]
                act.activation(Y[:, k % 2], yp, ACT.Copy, scale=weight).then_inc(yo_done, 1)

            def batch(b, first, last):
                r0 = None if first else (b - 1) * RT
                if not first:
                    columns(r0, 0)
                for hg in range(HG):
                    g = b * HG + hg
                    for n in range(PIECES):
                        here = units_at(n, B0U if first else BU)
                        for j in here:
                            v = hg * B0U + j if first else SU + r0 + hg * BU + j
                            gates(v)
                        exps(g, n)
                        for j in units_at(n - 1, B0U if first else BU):
                            high_part(hg * B0U + j if first else SU + r0 + hg * BU + j, j % 2)
                        for j in here:
                            k = hg * BU + j
                            if not first and k:
                                routed_out(b, k - 1)
                            if not first and k + 1 < RT:
                                columns(r0 + k + 1, (k + 1) % 2)
                if not first:
                    routed_out(b, RT - 1)

            over_batches(batch)


_INS = ["L0_attn_x", "L0_attn_Wq", "L0_attn_bq", "L0_attn_Wk", "L0_attn_bk", "L0_attn_Wv", "L0_attn_bv",
        "L0_attn_Wo", "L0_attn_bo", "L0_ffn_gate_w", "L0_ffn_w_gate", "L0_ffn_w_up", "L0_ffn_w_down",
        "L0_ffn_sw_gate", "L0_ffn_sw_up", "L0_ffn_sw_down"]


def kernel(**inputs):
    import numpy as _np
    import concourse.bacc as _bacc
    from concourse import mybir as _mybir
    from concourse.bass_utils import run_bass_kernel_spmd as _run

    nc = _bacc.Bacc("TRN2", target_bir_lowering=False, num_devices=1)
    arrays, args = {}, []
    for name in _INS:
        a = _np.ascontiguousarray(inputs[name])
        arrays[name] = a
        args.append(nc.dram_tensor(name, a.shape, _mybir.dt.from_np(a.dtype), kind="ExternalInput").ap())
    b, n, d = inputs["L0_attn_x"].shape
    args.append(nc.dram_tensor("out_0", (b * n + P, d), _mybir.dt.from_np(_np.dtype("float32")),
                               kind="ExternalOutput").ap())
    token_mixer_with_experts(nc, *args)
    r = _run(nc, [arrays], core_ids=[0])
    return r.results[0]["out_0"][:b * n].reshape(b, n, d)
```

```python
from contextlib import ExitStack

import concourse.bass as bass
from concourse import mybir

F32 = mybir.dt.float32
F16 = mybir.dt.float16
BF16 = mybir.dt.bfloat16
I32 = mybir.dt.int32
U32 = mybir.dt.uint32
ALU = mybir.AluOpType
ACT = mybir.ActivationFunctionType
AX = mybir.AxisListType
P = 128

XS = 64.0
WS = 256.0
HS = 8.0
PASSES = [(0, 0), (0, 1), (1, 0)]
Q_RUNS = [(0, 0, 2), (2, 0, 1), (3, 0, 3)]
K_RUNS = [(0, 0, 2), (2, 1, 2), (4, 0, 1), (5, 0, 1)]
TERMS = 6
MASKED = -1e30
LN_EPS = 1e-5


def token_mixer_with_experts(nc, x, wq, bq, wk, bk, wv, bv, wo, bo,
                             gate_w, w_gate, w_up, w_down, sw_gate, sw_up, sw_down, out):
    B, N, D = x.shape
    T = B * N
    E, _, I = w_gate.shape
    SH = sw_gate.shape[1] // I
    EW = E + SH
    H, DK = 16, D // 16
    TOPK = 4
    HC = D // P
    IP = I // 2
    TT = T // P
    CH = 512
    NCH = T // CH
    TPC = CH // P
    HG = H // 4
    NG = B * HG
    KT = N // P
    QC = N // CH
    UT = T * TOPK // P + E
    RS = UT * P
    STK = TERMS * DK
    STM = STK + 3
    assert D == 256 and N % CH == 0 and I % 2 == 0 and DK == 16

    nc.disable_value_cache = True
    xf = x.rearrange("b n d -> (b n) d")

    xrow_d = nc.dram_tensor("xrow_d", (T + P, 2 * D), F16).ap()
    xcol_d = nc.dram_tensor("xcol_d", (TT, P, 4 * P), F16).ap()
    q_d = nc.dram_tensor("q_d", (B, 3, HG, DK, 4, N), BF16).ap()
    k_d = nc.dram_tensor("k_d", (B, 3, HG, DK, 4, N), BF16).ap()
    v_d = nc.dram_tensor("v_d", (T, H, 2 * DK), F32).ap()
    slot_d = nc.dram_tensor("slot_d", (RS, 2), I32).ap()
    rsum_d = nc.dram_tensor("rsum_d", (2, 4, N), F32).ap()

    keep = ExitStack()
    with keep:
        def alloc(ctx):
            def sb(name, shape, dt=F32):
                return ctx.enter_context(nc.sbuf_tensor(name, shape, dt))

            def ps(name, shape, dt=F32):
                return ctx.enter_context(nc.psum_tensor(name, shape, dt))

            def sem(name):
                return ctx.enter_context(nc.semaphore(name))
            return sb, ps, sem

        sb, _, _ = alloc(keep)
        ident16 = sb("ident16", [P, P], F16)
        identb = sb("identb", [P, P], BF16)
        ident = sb("ident", [P, P])
        gu_w = sb("gu_w", [P, EW, 2, HC, 2 * I], F16)
        dn_w = sb("dn_w", [IP, EW, 2, 2, D], F16)
        woP = sb("woP", [P, HG, D])
        maskq = sb("maskq", [P, P], BF16)
        maskk = sb("maskk", [P, P], BF16)
        logits = sb("logits", [P, TT, E])
        entry = sb("entry", [P, TT * TOPK, 2], I32)
        slot_i = sb("slot_i", [P, TT * TOPK], I32)
        tile_e = sb("tile_e", [1, UT], I32)

        s = Kernel()
        s.x, s.wq, s.bq, s.wk, s.bk, s.wv, s.bv, s.wo = x, wq, bq, wk, bk, wv, bv, wo
        s.bo, s.gate_w, s.w_gate, s.w_up, s.w_down, s.sw_gate, s.sw_up, s.sw_down = bo, gate_w, w_gate, w_up, w_down, sw_gate, sw_up, sw_down
        s.xf, s.out, s.xrow_d, s.xcol_d, s.q_d, s.k_d, s.v_d, s.slot_d = xf, out, xrow_d, xcol_d, q_d, k_d, v_d, slot_d
        s.rsum_d, s.alloc, s.ident16, s.identb, s.ident, s.gu_w, s.dn_w, s.woP = rsum_d, alloc, ident16, identb, ident, gu_w, dn_w, woP
        s.maskq, s.maskk, s.logits, s.entry, s.slot_i, s.tile_e, s.B, s.N = maskq, maskk, logits, entry, slot_i, tile_e, B, N
        s.D, s.T, s.E, s.I, s.SH, s.EW, s.H, s.DK = D, T, E, I, SH, EW, H, DK
        s.TOPK, s.HC, s.IP, s.TT, s.CH, s.NCH, s.TPC, s.HG = TOPK, HC, IP, TT, CH, NCH, TPC, HG
        s.NG, s.KT, s.QC, s.UT, s.RS, s.STK, s.STM = NG, KT, QC, UT, RS, STK, STM
        prepare(nc, s)
        route(nc, s)
        attention_and_experts(nc, s)


class Kernel:
    pass


def wait_apart(eng, sem, value, passed):
    eng.wait_ge(sem, value)
    eng.sem_inc(passed, 1)


def prepare(nc, s):
    D, E, HC, H, DK, TT, TPC, CH, NCH = s.D, s.E, s.HC, s.H, s.DK, s.TT, s.TPC, s.CH, s.NCH
    I, IP, HG, SH = s.I, s.IP, s.HG, s.SH
    MO = D // P
    EPC = E // NCH
    assert EPC == SH == 2 and NCH % 2 == 0 and NCH >= 6 and s.QC == 2 and s.HG == 2 * MO
    with ExitStack() as ctx:
        sb, ps, sem = s.alloc(ctx)
        w32 = sb("w32", [P, 3, HC, D])
        g32 = sb("g32", [E, D])
        w16 = sb("w16", [P, 3, 2, HC, D], F16)
        gT32 = sb("gT32", [P, HC, E])
        g16 = sb("g16", [P, 2, HC, E], F16)
        bqk = sb("bqk", [P, 2, MO])
        bvb = sb("bvb", [P, D])
        gu = sb("gu_stage", [P, EPC, HC, 2, I])
        dn = sb("dn_stage", [IP, EPC, 2, D])
        X = sb("X", [P, 2, TPC, D])
        XN = sb("XN", [P, TPC, D])
        XR = sb("XR", [P, 2, TPC, 2, D], F16)
        XT = sb("XT", [P, 2, TPC, 2, HC, P], F16)
        st6 = sb("st6", [P, TPC, 6])
        mv = sb("mv", [P, TPC, 2])
        rv = sb("rv", [P, TPC])
        re_ = sb("re_", [P, TPC])
        rstd = sb("rstd", [P, TPC])
        nw = sb("nw", [P, 3, TPC])
        rfin = sb("rfin", [P, TPC])
        F = sb("F", [P, 2, CH])
        R1 = sb("R1", [P, 2, CH])
        F3 = sb("F3", [P, 4, 3, CH], BF16)
        V = sb("V", [P, TPC, H, 2 * DK])
        tp = [ps(f"tp{i}", [P, 2, 4 * P], F16) for i in range(2)]
        qk = [ps(f"qk{i}", [P, CH]) for i in range(2)]
        vp = [ps(f"vp{i}", [P, 2, D]) for i in range(2)]
        lg = ps("lg", [P, TPC, E])
        gt = ps("gt", [P, HC, E])

        sp_passed = sem("sp_passed"); dve_passed = sem("dve_passed")
        const_set = sem("const_set"); const_made = sem("const_made"); wo_clear = sem("wo_clear"); wo_in = sem("wo_in")
        gu_in = [sem(f"gu_in{i}") for i in range(EPC)]; hi_made = sem("hi_made"); lo_made = sem("lo_made")
        w_in = sem("w_in"); w_scaled = sem("w_scaled"); b_in = sem("b_in"); w_hi = sem("w_hi"); w_lo = sem("w_lo"); v_ones = sem("v_ones")
        gt_done = sem("gt_done"); gt_out = sem("gt_out")
        x_in = [sem("x_in0"), sem("x_in1")]
        stats = sem("stats"); aggr = sem("aggr"); ve_done = sem("ve_done"); rv_done = sem("rv_done")
        rstd_done = sem("rstd_done"); nw_done = sem("nw_done"); xn_done = sem("xn_done"); xhi = sem("xhi"); xlo = sem("xlo")
        turned = sem("turned"); xt_done = sem("xt_done")
        qk_done = sem("qk_done"); f1_done = sem("f1_done"); r1_done = sem("r1_done")
        f2_done = sem("f2_done"); f3_done = sem("f3_done"); v_done = sem("v_done"); v_out = sem("v_out")
        lg_done = sem("lg_done"); lg_out = sem("lg_out")
        xr_st = sem("xr_st"); xt_st = sem("xt_st"); qk_st = [sem(f"qk_st{i}") for i in range(4)]; v_st = sem("v_st")
        block = ctx.enter_context(nc.Block())

        def flat(w):
            return w.rearrange("p c n -> p (c n)")

        def over_steps(eng, step):
            for p in range(2):
                step(p, p, True, False)
            with eng.Fori(1, NCH // 2 - 1) as cc:
                for p in range(2):
                    step(cc * 2 + p, p, False, False)
            for p in range(2):
                step(NCH - 2 + p, p, False, True)

        def more(p, last):
            return not (last and p == 1)

        @block.sync
        def _(sp):
            for i, w in enumerate((s.wq, s.wk, s.wv)):
                sp.dma_start(w32[:, i], w.rearrange("(c p) n -> p c n", p=P)).then_inc(w_in, 16)
            sp.dma_start(g32[:, :], s.gate_w).then_inc(b_in, 16)
            for i, b in enumerate((s.bq, s.bk)):
                for hg in range(HG):
                    m, g = hg // 2, hg % 2
                    sp.dma_start(bqk[g * P // 2:(g + 1) * P // 2, i, m:m + 1],
                                 b.rearrange("(g h r o) -> g r h o", g=HG, h=4, o=1)[hg],
                                 allow_slow_non_contiguous=True).then_inc(b_in, 16)
            sp.dma_start(bvb[:, :], s.bv.rearrange("(a n) -> a n", a=1).broadcast_to([P, D])).then_inc(b_in, 16)
            sp.wait_ge(wo_clear, 1)
            for hg in range(HG):
                for h in range(4):
                    r = (4 * hg + h) * DK
                    sp.dma_start(s.woP[32 * h:32 * h + DK, hg, :], s.wo[r:r + DK, :]).then_inc(wo_in, 16)
            sp.dma_start(s.woP[DK:DK + 1, 0, :], s.bo.rearrange("(a n) -> a n", a=1)).then_inc(wo_in, 16)

            def store_rows(c, p):
                wait_apart(sp, xlo, TPC * (c + 1), sp_passed)
                sp.dma_start(s.xrow_d[bass.ds(c * CH, CH), :].rearrange("(j p) d -> p j d", p=P),
                             XR[:, p].rearrange("p j a d -> p j (a d)")).then_inc(xr_st, 16)

            def step(c, p, first, last):
                wait_apart(sp, xt_done, TPC * (c + 1), sp_passed)
                sp.dma_start(s.xcol_d[bass.ds(c * TPC, TPC)].rearrange("j p f -> p j f"),
                             XT[:, p].rearrange("p j a c t -> p j (a c t)")).then_inc(xt_st, 16)
                for i in range(4):
                    dst, m = (s.q_d, s.k_d)[i // MO], i % MO
                    b = c // 2 if isinstance(c, int) else (c - p) // 2
                    wait_apart(sp, f3_done, 4 * c + i + 1, sp_passed)
                    sp.dma_start(dst[bass.ds(b, 1), :, 2 * m:2 * m + 2, :, :, p * CH:(p + 1) * CH]
                                 .rearrange("o a g r h t -> (o g r h) a t"), F3[:, i]).then_inc(qk_st[i], 16)
                    if i == 0 and more(p, last):
                        store_rows(c + 1, 1 - p)
                wait_apart(sp, v_out, 2 * c + 2, sp_passed)
                sp.dma_start(s.v_d[bass.ds(c * CH, CH)].rearrange("(j p) h e -> p j (h e)", p=P),
                             V[:, :].rearrange("p j h e -> p j (h e)")).then_inc(v_st, 16)

            store_rows(0, 0)
            over_steps(sp, step)
            sp.wait_ge(wo_in, 16 * (4 * HG + 1))
            sp.wait_ge(xr_st, 16 * NCH)
            sp.wait_ge(xt_st, 16 * NCH)
            for i in range(4):
                sp.wait_ge(qk_st[i], 16 * NCH)
            sp.wait_ge(v_st, 16 * NCH)

        @block.gpsimd
        def _(pool):
            def load_x(p, src):
                pool.dma_start(X[:, p], src.rearrange("(j p) d -> p j d", p=P)).then_inc(x_in[p], 16)

            def load_expert(n, g, u, d):
                pool.dma_start(gu[:, n, :, 0, :], g.rearrange("(c p) i -> p c i", p=P)).then_inc(gu_in[n], 16)
                pool.dma_start(gu[:, n, :, 1, :], u.rearrange("(c p) i -> p c i", p=P)).then_inc(gu_in[n], 16)
                pool.dma_start(dn[:, n], d.rearrange("(c p) n -> p c n", p=IP)).then_inc(gu_in[n], 16)

            for p in range(2):
                load_x(p, s.xf[p * CH:(p + 1) * CH, :])
            for t in (s.ident16, s.identb, s.ident, s.maskq, s.maskk):
                last = pool.memset(t[:, :], 0.0)
            last.then_inc(const_set, 1)
            pool.wait_ge(const_set, 1)
            for t in (s.ident16, s.identb, s.ident):
                last = pool.affine_select(out=t[:, :], in_=t[:, :], compare_op=ALU.not_equal, fill=1.0, base=0,
                                          pattern=[[-1, P]], channel_multiplier=1)
            last.then_inc(const_made, 1)
            for n in range(SH):
                c = slice(n * I, (n + 1) * I)
                load_expert(n, s.sw_gate[:, c], s.sw_up[:, c], s.sw_down[c, :])
            pool.memset(V[:, :, :, DK:2 * DK], 1.0).then_inc(v_ones, 1)
            pool.memset(s.woP[:, :, :], 0.0).then_inc(wo_clear, 1)
            pool.affine_select(out=s.maskq[:, :], in_=s.maskq[:, :], compare_op=ALU.is_ge, fill=MASKED, base=0,
                               pattern=[[-1, P]], channel_multiplier=1)
            pool.affine_select(out=s.maskk[:, :], in_=s.maskk[:, :], compare_op=ALU.is_ge, fill=MASKED, base=0,
                               pattern=[[1, P]], channel_multiplier=-1).then_inc(const_made, 1)

            def step(c, p, first, last):
                if not last:
                    pool.wait_ge(xn_done, TPC * (c + 1))
                    load_x(p, s.xf[bass.ds((c + 2) * CH, CH), :])
                for n in range(EPC):
                    e = c * EPC + n
                    pool.wait_ge(lo_made, 2 * (c * EPC + n + 1))
                    load_expert(n, *(w[bass.ds(e, 1)].rearrange("o r c -> (o r) c") for w in (s.w_gate, s.w_up, s.w_down)))

            over_steps(pool, step)
            pool.wait_ge(const_made, 2)

        def one(t):
            return t.rearrange("p o c n -> p (o c) n")

        def expert_parts(c, n):
            e = slice(E + n, E + n + 1) if c is None else bass.ds(c * EPC + n, 1)
            return ([one(s.gu_w[:, e, a]).rearrange("p c (a i) -> p c a i", a=2) for a in range(2)],
                    [one(s.dn_w[:, e, a]) for a in range(2)])

        @block.scalar
        def _(act):
            def root(c):
                act.wait_ge(rv_done, c + 1)
                act.activation(rstd[:, :], rv[:, :], ACT.Sqrt, scale=XS * XS).then_inc(rstd_done, 1)

            def rows_high(c, p):
                for j in range(TPC):
                    act.wait_ge(xn_done, TPC * c + j + 1)
                    if j == 0 and not (isinstance(c, int) and c < 2):
                        act.wait_ge(xr_st, 16 * (c - 1))
                    act.activation(XR[:, p, j, 0], XN[:, j], ACT.Copy).then_inc(xhi, 1)

            def columns(c, p):
                for j in range(TPC):
                    if j % 2 == 0:
                        act.wait_ge(turned, TPC * c + j + 2)
                    if j == 0 and not (isinstance(c, int) and c < 2):
                        act.wait_ge(xt_st, 16 * (c - 1))
                        act.wait_ge(v_done, 2 * (c - 1))
                    act.activation(XT[:, p, j].rearrange("p a c t -> p (a c t)"), tp[j // 2][:, j % 2],
                                   ACT.Copy).then_inc(xt_done, 1)

            def weights_high(c, n):
                (gh, _), (dh, _) = expert_parts(c, n)
                done = 0 if c is None else c + 1
                act.wait_ge(gu_in[n], 48 * (done + 1))
                act.activation(gh, gu[:, n], ACT.Copy, scale=WS).then_inc(hi_made, 1)
                act.activation(dh, dn[:, n], ACT.Copy, scale=WS).then_inc(hi_made, 1)

            def product(c, i):
                act.wait_ge(qk_done, 4 * c + i + 1)
                bias = bqk[:, i // 2, i % MO:i % MO + 1]
                act.activation(F[:, i % 2], qk[i % 2][:, :], ACT.Identity, scale=1.0 / (XS * WS), bias=bias)
                if not (isinstance(c, int) and c == 0):
                    act.wait_ge(qk_st[i], 16 * c)
                act.activation(F3[:, i, 0], qk[i % 2][:, :], ACT.Identity, scale=1.0 / (XS * WS),
                               bias=bias).then_inc(f1_done, 1)

            def second_part(c, i):
                act.wait_ge(r1_done, 4 * c + i + 1)
                act.activation(F3[:, i, 1], R1[:, i % 2], ACT.Copy).then_inc(f2_done, 1)

            def step(c, p, first, last):
                product(c, 0)
                product(c, 1)
                if more(p, last):
                    root(c + 1)
                second_part(c, 0)
                if more(p, last):
                    rows_high(c + 1, 1 - p)
                weights_high(c, 0)
                product(c, 2)
                second_part(c, 1)
                product(c, 3)
                second_part(c, 2)
                second_part(c, 3)
                if more(p, last):
                    columns(c + 1, 1 - p)
                act.wait_ge(lg_done, c + 1)
                act.activation(s.logits[:, bass.ds(c * TPC, TPC), :], lg[:, :, :], ACT.Copy,
                               scale=1.0 / (XS * WS)).then_inc(lg_out, 1)
                weights_high(c, 1)

            root(0)
            act.wait_ge(w_in, 48)
            for i in range(2):
                for h in range(HC):
                    act.activation(F[:, i, h * D:(h + 1) * D].rearrange("p (g r h) -> p g r h", g=HG, h=4),
                                   w32[:, i, h].rearrange("p (g h r) -> p g r h", g=HG, h=4), ACT.Copy,
                                   scale=WS).then_inc(w_scaled, 1)
            for i in range(2):
                act.wait_ge(w_scaled, HC * (i + 1))
                act.activation(flat(w16[:, i, 0]), F[:, i], ACT.Copy).then_inc(w_hi, 1)
            act.activation(w16[:, 2, 0], w32[:, 2], ACT.Copy, scale=WS).then_inc(w_hi, 1)
            act.wait_ge(gt_out, 1)
            act.activation(g16[:, 0], gT32[:, :, :], ACT.Copy, scale=WS).then_inc(w_hi, 1)
            act.wait_ge(b_in, 16 * (2 * HG + 2))
            rows_high(0, 0)
            columns(0, 0)
            for n in range(SH):
                weights_high(None, n)
            over_steps(act, step)

        @block.vector
        def _(dve):
            def newton(c, i, ins):
                ins.then_inc(nw_done, 1)
                dve.wait_ge(nw_done, 4 * c + i + 1)

            def variances(c, p):
                dve.wait_ge(x_in[p], (c // 2 + 1) * 16 if isinstance(c, int) else (c + 2 - p) * 8)
                for j in range(TPC):
                    dve.bn_stats(st6[:, j], X[:, p, j]).then_inc(stats, 1)
                if not (isinstance(c, int) and c == 0):
                    dve.wait_ge(xn_done, TPC * c)
                for j in range(TPC):
                    wait_apart(dve, stats, TPC * c + j + 1, dve_passed)
                    dve.bn_aggr(mv[:, j], st6[:, j]).then_inc(aggr, 1)
                dve.wait_ge(aggr, TPC * (c + 1))
                dve.tensor_scalar(re_[:, :], mv[:, :, 1], LN_EPS, None, ALU.add).then_inc(ve_done, 1)
                dve.wait_ge(ve_done, c + 1)
                dve.reciprocal(rv[:, :], re_[:, :]).then_inc(rv_done, 1)

            def normalise(c, p):
                dve.wait_ge(rstd_done, c + 1)
                newton(c, 0, dve.tensor_tensor(nw[:, 0], rstd[:, :], rstd[:, :], ALU.mult))
                newton(c, 1, dve.tensor_tensor(nw[:, 1], nw[:, 0], re_[:, :], ALU.mult))
                newton(c, 2, dve.tensor_scalar(nw[:, 2], nw[:, 1], -0.5 / (XS * XS), 1.5, ALU.mult, ALU.add))
                newton(c, 3, dve.tensor_tensor(rfin[:, :], rstd[:, :], nw[:, 2], ALU.mult))
                if not (isinstance(c, int) and c == 0):
                    dve.wait_ge(xlo, TPC * c)
                for j in range(TPC):
                    dve.tensor_scalar(XN[:, j], X[:, p, j], mv[:, j, 0:1], rfin[:, j:j + 1],
                                      ALU.subtract, ALU.mult).then_inc(xn_done, 1)

            def rows_low(c, p):
                for j in range(TPC):
                    dve.wait_ge(xhi, TPC * c + j + 1)
                    dve.tensor_tensor(XR[:, p, j, 1], XN[:, j], XR[:, p, j, 0], ALU.subtract).then_inc(xlo, 1)

            def first_rest(c, i):
                if i >= 2 or not (isinstance(c, int) and c == 0):
                    dve.wait_ge(f3_done, 4 * c + i - 1)
                dve.wait_ge(f1_done, 4 * c + i + 1)
                dve.tensor_tensor(R1[:, i % 2], F[:, i % 2], F3[:, i, 0], ALU.subtract).then_inc(r1_done, 1)

            def third_part(c, i):
                dve.wait_ge(f2_done, 4 * c + i + 1)
                dve.tensor_tensor(F3[:, i, 2], R1[:, i % 2], F3[:, i, 1], ALU.subtract).then_inc(f3_done, 1)

            def values(c, i):
                dve.wait_ge(v_done, 2 * c + i + 1)
                if i == 0 and not (isinstance(c, int) and c == 0):
                    dve.wait_ge(v_st, 16 * c)
                dve.scalar_tensor_tensor(
                    out=V[:, 2 * i:2 * i + 2, :, 0:DK],
                    in0=vp[i][:, :, :].rearrange("p j (h e) -> p j h e", h=H), scalar=1.0 / (XS * WS),
                    in1=bvb[:, :].rearrange("p (a h e) -> p a h e", a=1, h=H).broadcast_to([P, 2, H, DK]),
                    op0=ALU.mult, op1=ALU.add).then_inc(v_out, 1)

            def weights_low(c, n):
                (gh, gl), (dh, dl) = expert_parts(c, n)
                done = n if c is None else SH + c * EPC + n
                dve.wait_ge(hi_made, 2 * done + 1)
                dve.scalar_tensor_tensor(out=gl, in0=gu[:, n], scalar=WS, in1=gh,
                                         op0=ALU.mult, op1=ALU.subtract).then_inc(lo_made, 1)
                dve.wait_ge(hi_made, 2 * done + 2)
                dve.scalar_tensor_tensor(out=dl, in0=dn[:, n], scalar=WS, in1=dh,
                                         op0=ALU.mult, op1=ALU.subtract).then_inc(lo_made, 1)

            def step(c, p, first, last):
                if more(p, last):
                    variances(c + 1, 1 - p)
                first_rest(c, 0)
                first_rest(c, 1)
                if more(p, last):
                    normalise(c + 1, 1 - p)
                third_part(c, 0)
                if more(p, last):
                    rows_low(c + 1, 1 - p)
                weights_low(c, 0)
                first_rest(c, 2)
                third_part(c, 1)
                first_rest(c, 3)
                third_part(c, 2)
                third_part(c, 3)
                values(c, 0)
                values(c, 1)
                weights_low(c, 1)

            variances(0, 0)
            normalise(0, 0)
            dve.wait_ge(gt_done, 1)
            dve.tensor_copy(gT32[:, :, :], gt[:, :, :]).then_inc(gt_out, 1)
            for i in range(2):
                dve.wait_ge(w_hi, i + 1)
                dve.tensor_tensor(flat(w16[:, i, 1]), F[:, i], flat(w16[:, i, 0]), ALU.subtract).then_inc(w_lo, 1)
            dve.wait_ge(w_hi, 3)
            dve.scalar_tensor_tensor(out=w16[:, 2, 1], in0=w32[:, 2], scalar=WS, in1=w16[:, 2, 0],
                                     op0=ALU.mult, op1=ALU.subtract).then_inc(w_lo, 1)
            dve.wait_ge(w_hi, 4)
            dve.scalar_tensor_tensor(out=g16[:, 1], in0=gT32[:, :, :], scalar=WS, in1=g16[:, 0],
                                     op0=ALU.mult, op1=ALU.subtract).then_inc(w_lo, 1)
            dve.wait_ge(b_in, 16 * (2 * HG + 2))
            dve.wait_ge(v_ones, 1)
            rows_low(0, 0)
            for n in range(SH):
                weights_low(None, n)
            over_steps(dve, step)

        @block.tensor
        def _(pe):
            def turn(c, p):
                for j in range(TPC):
                    pe.wait_ge(xlo, TPC * c + j + 1)
                    if j == 0 and not (isinstance(c, int) and c == 0):
                        pe.wait_ge(xt_done, TPC * c)
                    for a in range(2):
                        for h in range(HC):
                            o = (a * HC + h) * P
                            last = pe.transpose(tp[j // 2][:, j % 2, o:o + P],
                                                XR[:, p, j, a, h * P:(h + 1) * P], s.ident16[:, :])
                    last.then_inc(turned, 1)

            def step(c, p, first, last):
                began = not (isinstance(c, int) and c == 0)
                pe.wait_ge(xt_done, TPC * (c + 1))
                for i in range(4):
                    w, m = i // MO, i % MO
                    if i >= 2 or began:
                        pe.wait_ge(f1_done, 4 * c + i - 1)
                    n = 0
                    for a, b in PASSES:
                        for h in range(HC):
                            x = pe.matmul(qk[i % 2][:, :], w16[:, w, a, h, m * P:(m + 1) * P],
                                          XT[:, p, :, b, h], start=n == 0, stop=n == 2 * 3 - 1)
                            n += 1
                    x.then_inc(qk_done, 1)
                if more(p, last):
                    turn(c + 1, 1 - p)
                if began:
                    pe.wait_ge(lg_out, c)
                for j in range(TPC):
                    terms = [(a, b, h) for a in range(2) for b in range(2) for h in range(HC)]
                    for n, (a, b, h) in enumerate(terms):
                        x = pe.matmul(lg[:, j], XT[:, p, j, a, h], g16[:, b, h], start=n == 0,
                                      stop=n == len(terms) - 1)
                x.then_inc(lg_done, 1)
                for i in range(2):
                    if began:
                        pe.wait_ge(v_out, 2 * c)
                    for j in range(2):
                        n = 0
                        for a, b in PASSES:
                            for h in range(HC):
                                x = pe.matmul(vp[i][:, j], XT[:, p, 2 * i + j, a, h], w16[:, 2, b, h],
                                              start=n == 0, stop=n == 2 * 3 - 1)
                                n += 1
                    x.then_inc(v_done, 1)

            pe.wait_ge(b_in, 16 * (2 * HG + 2))
            pe.wait_ge(const_made, 1)
            for c in range(HC):
                last = pe.transpose(gt[:, c], g32[:, c * P:(c + 1) * P], s.ident[0:E, 0:E])
            last.then_inc(gt_done, 1)
            turn(0, 0)
            pe.wait_ge(w_lo, 4)
            over_steps(pe, step)


def route(nc, s):
    TT, E, TOPK, UT, RS = s.TT, s.E, s.TOPK, s.UT, s.RS
    with ExitStack() as ctx:
        sb, ps, sem = s.alloc(ctx)
        mx = sb("mx", [P, TT])
        sh = sb("sh", [P, TT, E])
        ex = sb("ex", [P, TT, E])
        sm = sb("sm", [P, TT])
        rs = sb("rs", [P, TT])
        sc = sb("sc", [P, TT, E])
        top8 = sb("top8", [P, TT, 8])
        idx8 = sb("idx8", [P, TT, 8], U32)
        idxf = sb("idxf", [P, TT, TOPK])
        iota_e = sb("iota_e", [P, E])
        hot = sb("hot", [P, TOPK, TT, E])
        m2 = sb("m2", [P, 2, TT, E])
        chosen = sb("chosen", [P, TT, E], F16)
        tsum = sb("tsum", [P, TT])
        trec = sb("trec", [P, TT])
        tri = sb("tri", [P, P], F16)
        ones = sb("ones", [P, P], F16)
        zero = sb("zero", [P, TT])
        csum = sb("csum", [P, E, TT])
        exc = sb("exc", [P, E, TT])
        total_i = sb("total_i", [P, E], I32)
        tiles_i = sb("tiles_i", [P, E], I32)
        tiles_f = sb("tiles_f", [P, E])
        tend = sb("tend", [P, E])
        base = sb("base", [P, E])
        place = sb("place", [P, TT, E])
        pk = sb("pk", [P, TOPK, TT, E])
        posf = sb("posf", [P, TT, TOPK])
        hi_i = sb("hi_i", [P, TT * TOPK], I32)
        hi_f = sb("hi_f", [P, TT * TOPK])
        pt_f = sb("pt_f", [P, TT * TOPK])
        slot_f = sb("slot_f", [P, TT * TOPK])
        UC = (UT + P - 1) // P
        iota_u = sb("iota_u", [P, UC])
        cmp = sb("cmp", [P, UC, E - 1])
        te = sb("te", [P, UC])
        te16 = sb("te16", [P, UC], F16)
        zslot = sb("zslot", [P, RS // P, 2], I32)
        zrow = sb("zrow", [P, 2 * s.D], F16)
        pos_i = sb("pos_i", [P, TT * TOPK], I32)
        rank_p = ps("rank_p", [P, TT, E])
        cnt_p = ps("cnt_p", [P, TT, E])
        te_p = ps("te_p", [1, UC, P])
        const = sem("r_const"); step = sem("r_step"); expd = sem("r_exp"); mm = sem("r_mm")
        routed = sem("routed"); zeroed = sem("zeroed"); c0 = sem("r_c0")
        block = ctx.enter_context(nc.Block())

        def per_token(t):
            return t[:, :].rearrange("p (t a) -> p t a", a=1).broadcast_to([P, TT, E])

        @block.gpsimd
        def _(pool):
            pool.memset(zslot[:, :, :], 0).then_inc(c0, 1)
            pool.memset(zrow[:, :], 0.0)
            pool.memset(ones[:, :], 1.0)
            pool.memset(zero[:, :], 0.0)
            pool.iota(iota_e[:, :], [[1, E]], base=0, channel_multiplier=0, allow_small_or_imprecise_dtypes=True)
            pool.iota(iota_u[:, :], [[P, UC]], base=0, channel_multiplier=1,
                      allow_small_or_imprecise_dtypes=True).then_inc(c0, 1)
            pool.wait_ge(c0, 2)
            pool.iota(zslot[:, :, 0], [[0, UT]], base=s.T, channel_multiplier=1)
            pool.iota(s.entry[:, :, 0], [[P, TT], [0, TOPK]], base=0, channel_multiplier=1).then_inc(c0, 1)
            pool.wait_ge(c0, 3)
            pool.dma_start(s.xrow_d[s.T:s.T + P, :], zrow[:, :]).then_inc(zeroed, 16)
            pool.affine_select(out=tri[:, :], in_=ones[:, :], compare_op=ALU.is_gt, fill=0.0, base=0,
                               pattern=[[1, P]], channel_multiplier=-1).then_inc(const, 1)
            pool.dma_start(s.slot_d.rearrange("(p r) a -> p (r a)", p=P),
                           zslot[:, :, :].rearrange("p r a -> p (r a)")).then_inc(zeroed, 16)
            pool.wait_ge(zeroed, 32)

        @block.scalar
        def _(act):
            act.wait_ge(step, 2)
            act.activation(ex[:, :, :], sh[:, :, :], ACT.Exp).then_inc(expd, 1)

        @block.tensor
        def _(pe):
            pe.wait_ge(const, 1)
            pe.wait_ge(mm, 1)
            pe.matmul(rank_p[:, :, :], tri[:, :], chosen[:, :, :], start=True, stop=True).then_inc(mm, 1)
            pe.matmul(cnt_p[:, :, :], ones[:, :], chosen[:, :, :], start=True, stop=True).then_inc(mm, 1)
            pe.wait_ge(mm, 4)
            for c in range(UC):
                last = pe.matmul(te_p[:, c], te16[:, c:c + 1], s.ident16[:, :], start=True, stop=True)
            last.then_inc(mm, 1)

        @block.vector
        def _(dve):
            done = [0]

            def then(ins):
                done[0] += 1
                ins.then_inc(step, 1)
                dve.wait_ge(step, done[0])

            then(dve.tensor_reduce(mx[:, :], s.logits[:, :, :], AX.X, ALU.max))
            then(dve.tensor_tensor(sh[:, :, :], s.logits[:, :, :], per_token(mx), ALU.subtract))
            dve.wait_ge(expd, 1)
            dve.wait_ge(const, 1)
            then(dve.tensor_reduce(sm[:, :], ex[:, :, :], AX.X, ALU.add))
            then(dve.reciprocal(rs[:, :], sm[:, :]))
            then(dve.tensor_tensor(sc[:, :, :], ex[:, :, :], per_token(rs), ALU.mult))
            for t in range(TT):
                last = dve.max(top8[:, t], sc[:, t])
            then(last)
            for t in range(TT):
                last = dve.max_index(idx8[:, t], top8[:, t], sc[:, t])
            then(last)
            then(dve.tensor_copy(idxf[:, :, :], idx8[:, :, 0:TOPK]))
            then(dve.tensor_reduce(tsum[:, :], top8[:, :, 0:TOPK], AX.X, ALU.add))
            then(dve.reciprocal(trec[:, :], tsum[:, :]))
            then(dve.scalar_tensor_tensor(out=s.entry[:, :, :].bitcast(F32)[:, :, 1].rearrange("p (t k) -> p t k", k=TOPK),
                                          in0=top8[:, :, 0:TOPK], scalar=1.0 / (HS * WS),
                                          in1=trec[:, :].rearrange("p (t a) -> p t a", a=1)
                                          .broadcast_to([P, TT, TOPK]), op0=ALU.mult, op1=ALU.mult))
            then(dve.tensor_tensor(hot[:, :, :, :], idxf[:, :, :].rearrange("p t (k a) -> p k t a", a=1)
                                   .broadcast_to([P, TOPK, TT, E]),
                                   iota_e[:, :].rearrange("p (a b e) -> p a b e", a=1, b=1)
                                   .broadcast_to([P, TOPK, TT, E]), ALU.is_equal))
            then(dve.tensor_tensor(m2[:, :, :, :], hot[:, 0:2], hot[:, 2:4], ALU.add))
            dve.tensor_tensor(chosen[:, :, :], m2[:, 0], m2[:, 1], ALU.add).then_inc(mm, 1)
            dve.wait_ge(mm, 3)
            for e in range(E):
                last = dve.tensor_tensor_scan(csum[:, e], cnt_p[:, :, e], zero[:, :], 0.0, ALU.add, ALU.add)
            then(last)
            then(dve.tensor_tensor(exc[:, :, :], csum[:, :, :], cnt_p[:, :, :].rearrange("p t e -> p e t"), ALU.subtract))
            then(dve.tensor_scalar(total_i[:, :], csum[:, :, TT - 1], float(P - 1), None, ALU.add))
            then(dve.tensor_scalar(tiles_i[:, :], total_i[:, :], 7, None, ALU.arith_shift_right))
            then(dve.tensor_copy(tiles_f[:, :], tiles_i[:, :]))
            then(dve.tensor_tensor_scan(tend[:, :], tiles_f[:, :], zero[:, 0:E], 0.0, ALU.add, ALU.add))
            then(dve.tensor_tensor(cmp[:, :, :],
                                   iota_u[:, :].rearrange("p (u a) -> p u a", a=1).broadcast_to([P, UC, E - 1]),
                                   tend[:, 0:E - 1].rearrange("p (a e) -> p a e", a=1).broadcast_to([P, UC, E - 1]),
                                   ALU.is_ge))
            then(dve.tensor_reduce(te[:, :], cmp[:, :, :], AX.X, ALU.add))
            dve.tensor_copy(te16[:, :], te[:, :]).then_inc(mm, 1)
            then(dve.tensor_tensor(base[:, :], tend[:, :], tiles_f[:, :], ALU.subtract))
            then(dve.tensor_scalar(base[:, :], base[:, :], float(P), None, ALU.mult))
            then(dve.tensor_tensor(place[:, :, :], rank_p[:, :, :], exc[:, :, :].rearrange("p e t -> p t e"), ALU.add))
            then(dve.tensor_tensor(place[:, :, :], place[:, :, :],
                                   base[:, :].rearrange("p (a e) -> p a e", a=1).broadcast_to([P, TT, E]), ALU.add))
            then(dve.tensor_tensor(pk[:, :, :, :], place[:, :, :].rearrange("p (a t) e -> p a t e", a=1)
                                   .broadcast_to([P, TOPK, TT, E]), hot[:, :, :, :], ALU.mult))
            then(dve.tensor_reduce(posf[:, :, :].rearrange("p t k -> p k t"), pk[:, :, :, :], AX.X, ALU.add))
            pf = posf[:, :, :].rearrange("p t k -> p (t k)")
            then(dve.tensor_copy(pos_i[:, :], pf))
            then(dve.tensor_scalar(hi_i[:, :], pos_i[:, :], 7, None, ALU.arith_shift_right))
            then(dve.tensor_copy(hi_f[:, :], hi_i[:, :]))
            then(dve.tensor_scalar(pt_f[:, :], pf, float(UT), None, ALU.mult))
            then(dve.scalar_tensor_tensor(out=slot_f[:, :], in0=hi_f[:, :], scalar=1.0 - P * UT, in1=pt_f[:, :],
                                          op0=ALU.mult, op1=ALU.add))
            then(dve.tensor_copy(s.slot_i[:, :], slot_f[:, :]))
            dve.wait_ge(mm, 5)
            dve.tensor_copy(s.tile_e[:, :], te_p[:, :, :].rearrange("p c t -> p (c t)")[:, 0:UT]).then_inc(routed, 1)


def attention_and_experts(nc, s):
    D, N, B, H, DK, HG, NG, KT, QC, CH, TT = s.D, s.N, s.B, s.H, s.DK, s.HG, s.NG, s.KT, s.QC, s.CH, s.TT
    STK, STM = s.STK, s.STM
    E, SH, I, IP, HC, UT, TOPK, T = s.E, s.SH, s.I, s.IP, s.HC, s.UT, s.TOPK, s.T
    with ExitStack() as ctx:
        sb, ps, sem = s.alloc(ctx)
        Qs = sb("Qs", [STM, 2, 4, N], BF16)
        Ks = sb("Ks", [STM, 2, 4, N], BF16)
        Vs = sb("Vs", [P, 2, KT, 4, 2 * DK])
        PB = 3
        probs = sb("probs", [P, PB, 4 * CH])
        part = sb("part", [P, 2, 2, 4, KT])
        rmax = sb("rmax", [P, 2, 4 * KT])
        nm = sb("nm", [4 * KT, 2, 3, P], BF16)
        nres = sb("nres", [4 * KT, P])
        oe = sb("oe", [P, QC, CH])
        sums = sb("sums", [P, 4 * N // P])
        recs = sb("recs", [P, 4 * N // P])
        rb = sb("rb", [P, QC, CH])
        OT = sb("OT", [P, HG, N])
        YB = 4
        YA = sb("YA", [P, YB, D])
        slots = sb("slots", [P, UT, 2], I32)
        GB, AHEAD = 6, 4
        idx = sb("idx", [P, GB], I32)
        XG = sb("XG", [P, GB, 2, HC, P], F16)
        XC = sb("XC", [P, 2, 2, HC, P], F16)
        xs = sb("xs", [P, 2, D])
        th = sb("th", [P, I])
        sg = sb("sg", [P, I])
        hf = sb("hf", [P, I])
        h16 = sb("h16", [IP, 2, 2, 2, P], F16)
        Y = sb("Y", [P, 2, D])
        smp = [ps(f"smp{i}", [P, CH]) for i in range(2)]
        stp = [ps(f"stp{i}", [P, CH]) for i in range(2)]
        pvp = ps("pvp", [P, CH])
        gup = ps("gup", [P, CH])
        turn = ps("turn", [P, CH])
        outs = ps("outs", [P, 2, D])
        xp = turn[:, 0:2 * P].bitcast(F16)
        hp = turn[0:IP, 0:2 * P]
        mxp = turn[0:4 * KT, 2 * P:3 * P]
        yp = outs[:, 0]
        wop = outs[:, 1]
        last_tiles = [bank[:, 0:D] for bank in smp + stp + [gup, turn]] + [yp, pvp[:, 0:D]]
        last_rows = probs[:, 0].rearrange("p (t d) -> p t d", t=KT)

        PIECES = 38
        SU = TT * SH
        NV = SU + UT
        B0U = SU // HG
        BU = UT // (NG - HG)

        def max_pieces():
            out = []
            for t in range(KT):
                for k0 in range(0, (t + 1) * P, CH):
                    w = min(CH, (t + 1) * P - k0)
                    n = CH // w if w in (128, 256, 512) else 1
                    for h in range(0, 4, n):
                        out.append((t, k0, w, h, n))
            assert len(out) == PIECES
            return out

        def key_steps():
            return [(q, t, max(0, t * P - q * CH)) for q in range(QC) for t in range((q + 1) * CH // P)]

        def score_pieces():
            out = []
            for n, (q, t, q0) in enumerate(key_steps()):
                w = CH - q0
                m = CH // w if w in (128, 256, 512) else 1
                for h in range(0, 4, m):
                    out.append((n, h, m))
            assert len(out) == PIECES
            return out

        MAXP, STEPS, SCP = max_pieces(), key_steps(), score_pieces()
        NST = len(STEPS)
        MAX_FROM, MAX_TO = 3, 30
        TURN = 31
        RECIPS, FINISH, OUT0 = 4, 10, 12
        RT = HG * BU
        ADDS = RT + KT

        def next_pieces(n):
            a = (n - MAX_FROM) * PIECES // (MAX_TO - MAX_FROM)
            z = (n - MAX_FROM + 1) * PIECES // (MAX_TO - MAX_FROM)
            return range(max(0, min(a, PIECES)), max(0, min(z, PIECES)))

        def units_at(n, many):
            return [j for j in range(many) if j * (PIECES - 2) // many == n]

        def tiles_at(n):
            return [t for t in range(KT) if 14 + 3 * t == n]

        ADD_AT = [5, 6, 8, 9, 11, 13, 15, 17]
        assert len(ADD_AT) == KT

        def added_before(b, k):
            return 1 + (b - 1) * ADDS + k + sum(a < k for a in ADD_AT)

        qk_in = [sem("qk_in0"), sem("qk_in1")]
        v_in = [sem("v_in0"), sem("v_in1")]
        a_const = sem("a_const"); a_ones = sem("a_ones")
        smax_done = sem("smax_done"); red_done = sem("red_done"); rmax_done = sem("rmax_done")
        mT_done = sem("mT_done"); nm_a = sem("nm_a"); nm_done = sem("nm_done"); nm_in = sem("nm_in")
        st_done = sem("st_done"); exp_done = sem("exp_done"); pv_done = sem("pv_done"); oe_done = sem("oe_done")
        sums_in = sem("sums_in"); rec_done = sem("rec_done"); rec_st = sem("rec_st"); rb_in = sem("rb_in")
        ot_done = sem("ot_done"); wo_done = sem("wo_done"); ya_done = sem("ya_done")
        scattered = sem("scattered"); sl_in = sem("sl_in"); idx_done = sem("idx_done")
        xg_in = [sem(f"xg_in{i}") for i in range(GB)]
        xc_in = [sem("xc_in0"), sem("xc_in1")]; xs_in = [sem("xs_in0"), sem("xs_in1")]
        xp_done = sem("xp_done"); xc_done = sem("xc_done"); gu_done = sem("gu_done"); th_done = sem("th_done")
        sg_done = sem("sg_done"); hf_done = sem("hf_done"); hT_done = sem("hT_done"); hh_done = sem("hh_done"); hl_done = sem("hl_done")
        y_done = sem("y_done"); yo_done = sem("yo_done"); out_st = [sem("out_st0"), sem("out_st1")]; added = sem("added")
        block = ctx.enter_context(nc.Block())

        def over_batches(batch):
            for b in range(B):
                batch(b, b == 0, b == B - 1)

        @block.gpsimd
        def _(pool):
            for b in range(2):
                pool.memset(part[:, b, 1], -3.0e38)
            pool.memset(YA[:, 0], 0.0).then_inc(a_const, 1)
            pool.wait_ge(a_const, 1)
            pool.memset(Ks[STK:STM], 1.0).then_inc(a_ones, 1)
            pool.dma_start(s.out[T:T + P, :], YA[:, 0]).then_inc(added, 16)
            for i in range(TT * TOPK):
                pool.indirect_dma_start(s.slot_d, bass.IndirectOffsetOnAxis(ap=s.slot_i[:, i:i + 1], axis=0),
                                        s.entry[:, i, :], None).then_inc(scattered, 16)
            pool.wait_ge(scattered, 16 * TT * TOPK)
            pool.dma_start(slots[:, :, :].rearrange("p u a -> p (u a)"),
                           s.slot_d.rearrange("(p u) a -> p (u a)", p=P)).then_inc(sl_in, 16)
            pool.wait_ge(sl_in, 16)
            pool.wait_ge(a_ones, 1)

            def gather(r, q):
                pool.tensor_copy(idx[:, q:q + 1], slots[:, r, 0:1]).then_inc(idx_done, 1)
                pool.wait_ge(idx_done, r + 1)
                pool.indirect_dma_start(XG[:, q].rearrange("p a c t -> p (a c t)"), None, s.xrow_d,
                                        bass.IndirectOffsetOnAxis(ap=idx[:, q:q + 1], axis=0)).then_inc(xg_in[q], 16)

            def scatter_add(b, k, r):
                pool.wait_ge(yo_done, r + TT + 1)
                pool.wait_ge(added, 16 * added_before(b, k))
                pool.indirect_dma_start(s.out, bass.IndirectOffsetOnAxis(ap=idx[:, k % GB:k % GB + 1], axis=0),
                                        Y[:, k % 2], None, compute_op=ALU.add).then_inc(added, 16)

            def add_attention(tile, t, adds):
                pool.wait_ge(ya_done, tile + 1)
                pool.wait_ge(added, 16 * adds)
                pool.dma_start(s.out[tile * P:(tile + 1) * P, :], YA[:, t % YB], accum_op=ALU.add).then_inc(added, 16)

            for r in range(AHEAD):
                gather(r, r % GB)
            for i in range(2):
                pool.wait_ge(out_st[i], 16 * TT // 2)

            def batch(b, last):
                for k in range(RT):
                    r = (b - 1) * RT + k
                    if not last or k + AHEAD < RT:
                        gather(r + AHEAD, (k + AHEAD) % GB)
                    scatter_add(b, k, r)
                    if k in ADD_AT:
                        t = ADD_AT.index(k)
                        add_attention((b - 1) * KT + t, t, added_before(b, k) + 1)

            for b in range(1, B):
                batch(b, b == B - 1)
            pool.wait_ge(added, 16 * (1 + UT + TT - KT))
            for q in range(QC):
                tile = TT - KT + q * KT // QC
                pool.wait_ge(ya_done, tile + KT // QC)
                pool.dma_start(s.out[tile * P:tile * P + CH, :].rearrange("(t p) d -> p t d", p=P),
                               last_rows[:, q * KT // QC:(q + 1) * KT // QC], accum_op=ALU.add).then_inc(added, 16)
            pool.wait_ge(added, 16 * (1 + UT + TT - KT + QC))

        @block.sync
        def _(sp):
            def load_group(b, hg, p, g):
                t0 = b * N
                for dst, src, runs in ((Ks, s.k_d, K_RUNS), (Qs, s.q_d, Q_RUNS)):
                    for n, a, k in runs:
                        sp.dma_start(dst[n * DK:(n + k) * DK, p].rearrange("r h t -> r (h t)"),
                                     src[b, a:a + k, hg].rearrange("a r h t -> a r (h t)")).then_inc(qk_in[p], 16)
                if g:
                    sp.wait_ge(pv_done, NST * g)
                sp.dma_start(Vs[:, p].rearrange("p k h e -> p k (h e)"),
                             s.v_d[t0:t0 + N, 4 * hg:4 * hg + 4, :]
                             .rearrange("(k p) h e -> p k (h e)", p=P)).then_inc(v_in[p], 16)

            def send_max(g, p):
                sp.wait_ge(nm_done, g + 1)
                for a in range(3):
                    sp.dma_start(Qs[STK + a:STK + a + 1, p].rearrange("o h (t q) -> o (h t) q", q=P),
                                 nm[:, p, a, :]).then_inc(nm_in, 16)

            def send_sums(g, q2):
                sp.wait_ge(oe_done, QC * (g + 1))
                for h in range(4):
                    sp.dma_start(sums[32 * h:32 * h + 32, :],
                                 oe[32 * h + DK:32 * h + DK + 1].rearrange("o q (p c) -> o (q p) c", p=32 // QC))\
                        .then_inc(sums_in, 16)
                sp.wait_ge(rec_done, g + 1)
                sp.dma_start(s.rsum_d[q2].rearrange("h (p c) -> (h p) c", p=32), recs[:, :]).then_inc(rec_st, 16)
                sp.wait_ge(rec_st, 16 * (g + 1))
                for h in range(4):
                    sp.dma_start(rb[32 * h:32 * h + 32].rearrange("p q c -> p (q c)"),
                                 s.rsum_d[q2, h:h + 1, :].broadcast_to([32, N])).then_inc(rb_in, 16)

            def shared_columns(t):
                if t >= 2:
                    sp.wait_ge(gu_done, SH * (t - 1))
                sp.dma_start(XC[:, t % 2].rearrange("p a c t -> p (a c t)"), s.xcol_d[t]).then_inc(xc_in[t % 2], 16)

            def shared_rows(t):
                if t >= 2:
                    sp.wait_ge(yo_done, t - 1)
                sp.dma_start(xs[:, t % 2], s.xf[t * P:(t + 1) * P, :]).then_inc(xs_in[t % 2], 16)

            def store_shared(t):
                sp.wait_ge(yo_done, t + 1)
                sp.dma_start(s.out[t * P:(t + 1) * P, :], Y[:, t % 2]).then_inc(out_st[t % 2], 16)

            def shared_tiles(begin, end):
                for t in range(max(0, begin), end):
                    if t + 2 < TT:
                        shared_columns(t + 2)
                    store_shared(t)
                    if t + 2 < TT:
                        shared_rows(t + 2)

            def batch(b, first, last):
                for hg in range(HG):
                    g = b * HG + hg
                    p = hg % 2
                    if first and hg:
                        shared_columns(hg * (B0U // SH) + 1)
                    if not (last and hg == HG - 1):
                        if g:
                            sp.wait_ge(st_done, PIECES * g)
                        load_group(b if hg < HG - 1 else b + 1, (hg + 1) % HG, 1 - p, g)
                    if first and hg:
                        store_shared(hg * (B0U // SH) - 1)
                        shared_rows(hg * (B0U // SH) + 1)
                    if not (first and hg == 0):
                        send_sums(g - 1, 1 - p)
                    if first:
                        shared_tiles(hg * (B0U // SH), (hg + 1) * (B0U // SH) - 1)
                    if not (last and hg == HG - 1):
                        send_max(g + 1, 1 - p)
                if first:
                    shared_tiles(TT - 1, TT)

            load_group(0, 0, 0, 0)
            for t in range(2):
                shared_columns(t)
                shared_rows(t)
            send_max(0, 0)
            over_batches(batch)
            send_sums(NG - 1, 1)
            for i in range(2):
                sp.wait_ge(out_st[i], 16 * TT // 2)

        @block.tensor
        def _(pe):
            def max_piece(g, p, r, n):
                t, k0, w, h0, nh = MAXP[n]
                bank = smp[n % 2]
                if n == 0:
                    pe.wait_ge(qk_in[p], 16 * len(K_RUNS + Q_RUNS) * (r + 1))
                if PIECES * g + n >= 2:
                    pe.wait_ge(red_done, PIECES * g + n - 1)
                for i in range(nh):
                    h = h0 + i
                    diag = k0 + w == (t + 1) * P
                    last = pe.matmul(bank[:, i * w:(i + 1) * w], Qs[0:STK, p, h, t * P:(t + 1) * P],
                                     Ks[0:STK, p, h, k0:k0 + w], start=True, stop=not diag)
                    if diag:
                        last = pe.matmul(bank[:, (i + 1) * w - P:(i + 1) * w], s.identb[:, :], s.maskq[:, :],
                                         start=False, stop=True)
                last.then_inc(smax_done, 1)

            def turn_max(g, p, turned, units):
                pe.wait_ge(rmax_done, g + 1)
                if turned:
                    pe.wait_ge(xc_done, turned)
                if units:
                    pe.wait_ge(hl_done, units)
                pe.transpose(mxp, rmax[:, p, :], s.ident[:, :]).then_inc(mT_done, 1)

            def score_piece(g, p, n):
                st, h0, nh = SCP[n]
                q, t, q0 = STEPS[st]
                w = CH - q0
                bank = stp[n % 2]
                if n == 0:
                    pe.wait_ge(nm_in, 48 * (g + 1))
                if PIECES * g + n >= 2:
                    pe.wait_ge(exp_done, PIECES * g + n - 1)
                for i in range(nh):
                    h = h0 + i
                    diag = t * P >= q * CH
                    last = pe.matmul(bank[:, i * w:(i + 1) * w], Ks[:, p, h, t * P:(t + 1) * P],
                                     Qs[:, p, h, q * CH + q0:(q + 1) * CH], start=True, stop=not diag)
                    if diag:
                        last = pe.matmul(bank[:, i * w:i * w + P], s.identb[:, :], s.maskk[:, :],
                                         start=False, stop=True)
                last.then_inc(st_done, 1)

            def values(g, p, r, st):
                q, t, q0 = STEPS[st]
                w = CH - q0
                if st == 0:
                    pe.wait_ge(v_in[p], 16 * (r + 1))
                if t == 0 and g + q:
                    pe.wait_ge(oe_done, QC * g + q)
                lastp = max(n for n, x in enumerate(SCP) if x[0] == st)
                pe.wait_ge(exp_done, PIECES * g + lastp + 1)
                for h in range(4):
                    last = pe.matmul(pvp[32 * h:32 * h + 32, q0:CH], Vs[:, p, t, h, :],
                                     probs[:, st % PB, h * w:(h + 1) * w], start=t == 0,
                                     stop=t == (q + 1) * CH // P - 1, tile_position=(0, 32 * h))
                last.then_inc(pv_done, 1)

            def project_groups(bank, t, begin, end):
                for hg in range(begin, end):
                    last = pe.matmul(bank, OT[:, hg, t * P:(t + 1) * P], s.woP[:, hg, :],
                                     start=hg == 0, stop=hg == HG - 1)
                return last

            def project(tile, t, normal, youts):
                if t == 0:
                    pe.wait_ge(ot_done, normal)
                if tile:
                    pe.wait_ge(ya_done, tile)
                pe.wait_ge(yo_done, youts)
                project_groups(wop, t, 0, HG).then_inc(wo_done, 1)

            def turn_rows(b, k, maxima):
                r = (b - 1) * RT + k
                q = k % GB
                pe.wait_ge(xg_in[q], 16 * ((b - 1) * (RT // GB) + k // GB + 1))
                if maxima:
                    pe.wait_ge(nm_done, maxima)
                for a in range(2):
                    for h in range(HC):
                        o = (a * HC + h) * P
                        last = pe.transpose(xp[:, o:o + P], XG[:, q, a, h], s.ident16[:, :])
                last.then_inc(xp_done, 1)

            def expert_of(r):
                return pe.value_load(s.tile_e[0:1, r:r + 1], min_val=0, max_val=E - 1)

            def weights_of(t, e, *ix):
                if isinstance(e, int):
                    return t[(slice(None), e) + ix]
                return t[(slice(None), bass.ds(e, 1)) + ix].rearrange("p o i -> p (o i)")

            def gate_up(v, xb, e):
                if v:
                    pe.wait_ge(hf_done, v)
                n = 0
                for a, b in PASSES:
                    for h in range(HC):
                        last = pe.matmul(gup[:, 0:2 * I], XC[:, xb, a, h], weights_of(s.gu_w, e, b, h, slice(0, 2 * I)),
                                         start=n == 0, stop=n == 5)
                        n += 1
                last.then_inc(gu_done, 1)

            def turn_h(v, turned, maxima):
                pe.wait_ge(hf_done, v + 1)
                if turned:
                    pe.wait_ge(xc_done, turned)
                if maxima:
                    pe.wait_ge(nm_done, maxima)
                for c in range(2):
                    last = pe.transpose(hp[:, c * P:(c + 1) * P], hf[:, c * IP:(c + 1) * IP], s.ident[:, :])
                last.then_inc(hT_done, 1)

            def down(v, hb, e, begin, end):
                pe.wait_ge(hl_done, v + 1)
                n = 0
                for c in range(2):
                    for a, b in PASSES:
                        last = pe.matmul(yp, h16[:, hb, a, c], weights_of(s.dn_w, e, b, c, slice(0, D)),
                                         start=begin and n == 0, stop=end and n == 5)
                        n += 1
                last.then_inc(y_done, 1)

            def shared_down(v):
                if v >= SH and v % SH == 0:
                    pe.wait_ge(yo_done, v // SH)
                down(v, v % 2, E + v % SH, v % SH == 0, v % SH == SH - 1)

            def routed_down(b, k, e, projected):
                r = (b - 1) * RT + k
                pe.wait_ge(yo_done, TT + r)
                if projected:
                    pe.wait_ge(ya_done, projected)
                down(SU + r, k % 2, e, True, True)

            def batch(b, first, last):
                projected = 0
                turned = 0
                downs = 0
                units = 0
                many = B0U if first else BU
                e_before = None
                if not first:
                    r0 = (b - 1) * RT
                    pe.wait_ge(hl_done, SU + r0)
                    turn_rows(b, 0, 0)
                    e_here = expert_of(r0)
                    turned = 1
                for hg in range(HG):
                    g = b * HG + hg
                    p = hg % 2
                    more = not (last and hg == HG - 1)
                    r = b * (HG // 2) + hg // 2
                    nst = 0
                    for n in range(PIECES):
                        here = units_at(n, B0U if first else BU)
                        maxima = g + 2 if more and n > TURN else 0
                        for j in here:
                            if first:
                                v = hg * B0U + j
                                if v % SH == 0:
                                    pe.wait_ge(xc_in[v // SH % 2], 16 * (v // SH // 2 + 1))
                                gate_up(v, v // SH % 2, E + v % SH)
                            else:
                                k = hg * BU + j
                                pe.wait_ge(xc_done, r0 + k + 1)
                                gate_up(SU + r0 + k, k % 2, e_here)
                        if more:
                            for m in next_pieces(n)[:1]:
                                max_piece(g + 1, 1 - p, b * (HG // 2) + (hg + 1) // 2, m)
                        score_piece(g, p, n)
                        for j in here:
                            v = hg * B0U + j
                            k = hg * BU + j
                            if first and v:
                                shared_down(v - 1)
                            if not first and k:
                                routed_down(b, k - 1, e_before, (b - 1) * KT + projected if k <= BU and projected else 0)
                                downs += 1
                            if not first and k + 1 < RT:
                                turn_rows(b, k + 1, maxima)
                                turned += 1
                                e_next = expert_of(r0 + k + 1)
                        if more:
                            for m in next_pieces(n)[1:]:
                                max_piece(g + 1, 1 - p, b * (HG // 2) + (hg + 1) // 2, m)
                        if not first and hg == 0:
                            for t in tiles_at(n):
                                project((b - 1) * KT + t, t, QC * g, TT + r0 + downs)
                                projected += 1
                        while nst < NST and SCP[n][0] > nst:
                            values(g, p, r, nst)
                            nst += 1
                        for j in units_at(n - 1, many):
                            if first:
                                turn_h(hg * B0U + j, 0, maxima)
                            else:
                                turn_h(SU + r0 + hg * BU + j, r0 + turned, maxima)
                                e_before, e_here = e_here, e_next
                            units = hg * many + j + 1
                        if more and n == TURN:
                            turn_max(g + 1, 1 - p, 0 if first else r0 + turned, units if first else SU + r0 + units)
                    while nst < NST:
                        values(g, p, r, nst)
                        nst += 1
                if first:
                    shared_down(SU - 1)
                else:
                    routed_down(b, RT - 1, e_before, 0)

            for n in range(PIECES):
                max_piece(0, 0, 0, n)
            turn_max(0, 0, 0, 0)
            pe.wait_ge(a_ones, 1)
            over_batches(batch)
            pe.wait_ge(ot_done, QC * (NG - 1))
            over = [(red_done, PIECES * NG), None, (exp_done, PIECES * NG), None, (hf_done, SU + UT),
                    (hl_done, SU + UT), (yo_done, TT + UT), (oe_done, QC * NG)]
            for t in range(KT):
                if over[t]:
                    pe.wait_ge(*over[t])
                project_groups(last_tiles[t], t, 0, HG - 1)
            for t in range(KT):
                if t % (KT // QC) == 0:
                    pe.wait_ge(ot_done, QC * (NG - 1) + t // (KT // QC) + 1)
                project_groups(last_tiles[t], t, HG - 1, HG).then_inc(wo_done, 1)

        @block.vector
        def _(dve):
            def reduce_piece(g, p, n):
                t, k0, w, h0, nh = MAXP[n]
                dve.wait_ge(smax_done, PIECES * g + n + 1)
                dve.tensor_reduce(part[:, p, k0 // CH, h0:h0 + nh, t],
                                  smp[n % 2][:, 0:nh * w].rearrange("p (h k) -> p h k", h=nh), AX.X,
                                  ALU.max).then_inc(red_done, 1)

            def close_max(g, p):
                dve.wait_ge(red_done, PIECES * (g + 1))
                dve.tensor_tensor(rmax[:, p, :], part[:, p, 0].rearrange("p h t -> p (h t)"),
                                  part[:, p, 1].rearrange("p h t -> p (h t)"), ALU.max).then_inc(rmax_done, 1)
                dve.wait_ge(mT_done, g + 1)
                dve.tensor_scalar(nm[:, p, 0], mxp, -1.0, None, ALU.mult).then_inc(nm_a, 1)
                dve.wait_ge(nm_a, 3 * g + 1)
                dve.scalar_tensor_tensor(out=nres[:, :], in0=mxp, scalar=-1.0, in1=nm[:, p, 0], op0=ALU.mult,
                                         op1=ALU.subtract).then_inc(nm_a, 1)
                dve.wait_ge(nm_a, 3 * g + 2)
                dve.tensor_copy(nm[:, p, 1], nres[:, :]).then_inc(nm_a, 1)
                dve.wait_ge(nm_a, 3 * g + 3)
                dve.tensor_tensor(nm[:, p, 2], nres[:, :], nm[:, p, 1], ALU.subtract).then_inc(nm_done, 1)

            def out_chunk(g, q):
                dve.wait_ge(pv_done, NST * g + (CH // P if q == 0 else NST))
                dve.tensor_copy(oe[:, q], pvp[:, :]).then_inc(oe_done, 1)

            def reciprocals(g):
                dve.wait_ge(sums_in, 64 * (g + 1))
                dve.reciprocal(recs[:, :], sums[:, :]).then_inc(rec_done, 1)

            def normalise(g, hg):
                dve.wait_ge(rb_in, 64 * (g + 1))
                for q in range(QC):
                    dve.tensor_tensor(OT[:, hg, q * CH:(q + 1) * CH], rb[:, q], oe[:, q], ALU.mult).then_inc(ot_done, 1)

            def silu_times_up(v):
                dve.wait_ge(th_done, v + 1)
                dve.scalar_tensor_tensor(out=sg[:, :], in0=th[:, :], scalar=1.0, in1=gup[:, 0:I],
                                         op0=ALU.add, op1=ALU.mult).then_inc(sg_done, 1)
                dve.wait_ge(sg_done, v + 1)
                if v:
                    dve.wait_ge(hT_done, v)
                dve.scalar_tensor_tensor(out=hf[:, :], in0=sg[:, :], scalar=0.5 * HS / (XS * WS) ** 2,
                                         in1=gup[:, I:2 * I], op0=ALU.mult, op1=ALU.mult).then_inc(hf_done, 1)

            def low_part(v, hb):
                dve.wait_ge(hh_done, v + 1)
                dve.tensor_tensor(h16[:, hb, 1].rearrange("i c t -> i (c t)"), hp,
                                  h16[:, hb, 0].rearrange("i c t -> i (c t)"), ALU.subtract).then_inc(hl_done, 1)

            def shared_out(t):
                dve.wait_ge(y_done, SH * (t + 1))
                dve.wait_ge(xs_in[t % 2], 16 * (t // 2 + 1))
                if t >= 2:
                    dve.wait_ge(out_st[t % 2], 16 * (t // 2))
                dve.scalar_tensor_tensor(out=Y[:, t % 2], in0=yp, scalar=1.0 / (HS * WS), in1=xs[:, t % 2],
                                         op0=ALU.mult, op1=ALU.add).then_inc(yo_done, 1)

            def attention_out(tile, t, adds):
                dve.wait_ge(wo_done, tile + 1)
                dve.wait_ge(added, 16 * adds)
                dve.tensor_copy(YA[:, t % YB], wop).then_inc(ya_done, 1)

            def batch(b, first, last):
                many = B0U if first else BU
                for hg in range(HG):
                    g = b * HG + hg
                    p = hg % 2
                    more = not (last and hg == HG - 1)
                    for n in range(PIECES):
                        here = units_at(n, B0U if first else BU)
                        if more:
                            for m in next_pieces(n)[:1]:
                                reduce_piece(g + 1, 1 - p, m)
                        for j in here:
                            v = hg * B0U + j if first else SU + (b - 1) * RT + hg * BU + j
                            silu_times_up(v)
                        if more:
                            for m in next_pieces(n)[1:]:
                                reduce_piece(g + 1, 1 - p, m)
                        for j in here:
                            v = hg * B0U + j
                            if first and v % SH == 0 and v:
                                shared_out(v // SH - 1)
                        for j in units_at(n - 1, many):
                            low_part(hg * B0U + j if first else SU + (b - 1) * RT + hg * BU + j, j % 2)
                        if not first and hg == 0:
                            for t in tiles_at(n):
                                attention_out((b - 1) * KT + t, t,
                                              added_before(b, 0) if t < YB else added_before(b, ADD_AT[t - YB]) + 2)
                        if not (first and hg == 0):
                            if n == RECIPS:
                                reciprocals(g - 1)
                            if n == FINISH:
                                normalise(g - 1, (hg - 1) % HG)
                        if n == OUT0:
                            out_chunk(g, 0)
                        if more and n == TURN:
                            close_max(g + 1, 1 - p)
                    out_chunk(g, 1)
                if first:
                    shared_out(TT - 1)

            dve.wait_ge(a_const, 1)
            for n in range(PIECES):
                reduce_piece(0, 0, n)
            close_max(0, 0)
            over_batches(batch)
            reciprocals(NG - 1)
            normalise(NG - 1, HG - 1)
            for t in range(KT):
                dve.wait_ge(wo_done, TT - KT + t + 1)
                dve.tensor_copy(last_rows[:, t], last_tiles[t]).then_inc(ya_done, 1)

        @block.scalar
        def _(act):
            def exps(g, n):
                st, h0, nh = SCP[n]
                w = CH - STEPS[st][2]
                act.wait_ge(st_done, PIECES * g + n + 1)
                if h0 == 0 and NST * g + st >= PB:
                    act.wait_ge(pv_done, NST * g + st - PB + 1)
                act.activation(probs[:, st % PB, h0 * w:(h0 + nh) * w], stp[n % 2][:, 0:nh * w], ACT.Exp,
                               scale=float(DK) ** -0.5).then_inc(exp_done, 1)

            def gates(v):
                act.wait_ge(gu_done, v + 1)
                if v:
                    act.wait_ge(sg_done, v)
                act.activation(th[:, :], gup[:, 0:I], ACT.Tanh, scale=0.5 / (XS * WS)).then_inc(th_done, 1)

            def high_part(v, hb):
                act.wait_ge(hT_done, v + 1)
                if v >= 2:
                    act.wait_ge(y_done, v - 1)
                act.activation(h16[:, hb, 0].rearrange("i c t -> i (c t)"), hp, ACT.Copy).then_inc(hh_done, 1)

            def columns(r, q):
                act.wait_ge(xp_done, r + 1)
                act.wait_ge(gu_done, SU + r - 1)
                act.activation(XC[:, q].rearrange("p a c t -> p (a c t)"), xp, ACT.Copy).then_inc(xc_done, 1)

            def routed_out(b, k):
                r = (b - 1) * RT + k
                act.wait_ge(y_done, SU + r + 1)
                if k == 0:
                    act.wait_ge(sl_in, 16)
                    for i in range(2):
                        act.wait_ge(out_st[i], 16 * TT // 2)
                act.wait_ge(added, 16 * (added_before(b, 0) if k < 2 else added_before(b, k - 2) + 1))
                weight = slots[:, :, :].bitcast(F32)[:, r, 1:2]
                act.activation(Y[:, k % 2], yp, ACT.Copy, scale=weight).then_inc(yo_done, 1)

            def batch(b, first, last):
                r0 = None if first else (b - 1) * RT
                if not first:
                    columns(r0, 0)
                for hg in range(HG):
                    g = b * HG + hg
                    for n in range(PIECES):
                        here = units_at(n, B0U if first else BU)
                        for j in here:
                            v = hg * B0U + j if first else SU + r0 + hg * BU + j
                            gates(v)
                        exps(g, n)
                        for j in units_at(n - 1, B0U if first else BU):
                            high_part(hg * B0U + j if first else SU + r0 + hg * BU + j, j % 2)
                        for j in here:
                            k = hg * BU + j
                            if not first and k:
                                routed_out(b, k - 1)
                            if not first and k + 1 < RT:
                                columns(r0 + k + 1, (k + 1) % 2)
                if not first:
                    routed_out(b, RT - 1)

            over_batches(batch)


_INS = ["L0_attn_x", "L0_attn_Wq", "L0_attn_bq", "L0_attn_Wk", "L0_attn_bk", "L0_attn_Wv", "L0_attn_bv",
        "L0_attn_Wo", "L0_attn_bo", "L0_ffn_gate_w", "L0_ffn_w_gate", "L0_ffn_w_up", "L0_ffn_w_down",
        "L0_ffn_sw_gate", "L0_ffn_sw_up", "L0_ffn_sw_down"]


def kernel(**inputs):
    import numpy as _np
    import concourse.bacc as _bacc
    from concourse import mybir as _mybir
    from concourse.bass_utils import run_bass_kernel_spmd as _run

    nc = _bacc.Bacc("TRN2", target_bir_lowering=False, num_devices=1)
    arrays, args = {}, []
    for name in _INS:
        a = _np.ascontiguousarray(inputs[name])
        arrays[name] = a
        args.append(nc.dram_tensor(name, a.shape, _mybir.dt.from_np(a.dtype), kind="ExternalInput").ap())
    b, n, d = inputs["L0_attn_x"].shape
    args.append(nc.dram_tensor("out_0", (b * n + P, d), _mybir.dt.from_np(_np.dtype("float32")),
                               kind="ExternalOutput").ap())
    token_mixer_with_experts(nc, *args)
    r = _run(nc, [arrays], core_ids=[0])
    return r.results[0]["out_0"][:b * n].reshape(b, n, d)
```
